# Optimizing a Trainium2 kernel written in Bass

```python
import numpy as np
import jax
import jax.numpy as jnp

def _softmax(x, axis=-1):
    return jax.nn.softmax(x, axis=axis)

def _gelu(x):
    return jax.nn.gelu(x, approximate=True)

def _silu(x):
    return jax.nn.silu(x)

def _sigmoid(x):
    return jax.nn.sigmoid(x)

def _layernorm(x, axis=-1, eps=1e-05):
    m = jnp.mean(x, axis=axis, keepdims=True)
    v = jnp.var(x, axis=axis, keepdims=True)
    return (x - m) / jnp.sqrt(v + eps)

def _scatter_add(tgt, idx, src, axis=0):
    return tgt.at[idx].add(src)

def _segment_sum(src, seg, n):
    return jax.ops.segment_sum(src, seg, n)
kernel_name = 'mk_adaln_d1_jaxref_r8_1a29f8'

def setup_inputs(seed: int=0):
    np.random.seed(seed)
    _w = jnp.asarray

    def _L0_attn_setup():
        import jax, jax.numpy as jnp
        import numpy as np
        B, T, D, H, FFN = (2, 256, 128, 16, 512)
        K = D // H
        EPS = 1e-06
        LN_EPS = 1e-05
        LAM_MIN = 1e-08

        def _ln(x, w, b):
            m = x.mean(-1, keepdims=True)
            v = ((x - m) ** 2).mean(-1, keepdims=True)
            return (x - m) * jax.lax.rsqrt(v + LN_EPS) * w + b

        def _lion(phi_q, phi_k, v, lam):
            b, h, t, kk = phi_q.shape
            kv = v.shape[-1]
            to_t = lambda a: a.transpose(2, 0, 1, 3)
            qt, kt, vt, lt = (to_t(phi_q), to_t(phi_k), to_t(v), to_t(lam))
            S0 = jnp.zeros((b, h, kk, kv), phi_q.dtype)

            def fwd(S, inp):
                q_t, k_t, v_t, l_t = inp
                S = S * l_t[..., None] + k_t[..., None] * v_t[..., None, :]
                return (S, jnp.einsum('bhk,bhkv->bhv', q_t, S))
            _, out_f = jax.lax.scan(fwd, S0, (qt, kt, vt, lt))
            q_shift = jnp.concatenate([qt[:1], qt[:-1]], axis=0)

            def bwd(R, inp):
                qs_t, k_t, v_t, l_t = inp
                R = l_t[..., None] * (k_t[..., None] * v_t[..., None, :] + R)
                return (R, jnp.einsum('bhk,bhkv->bhv', qs_t, R))
            _, out_b = jax.lax.scan(bwd, S0, (q_shift, kt, vt, lt), reverse=True)
            out_b = jnp.concatenate([out_b[1:], jnp.zeros_like(out_b[:1])], axis=0)
            return (out_f + out_b).transpose(1, 2, 0, 3)
        key = jax.random.key(seed)
        ks = jax.random.split(key, 12)
        s = 0.02
        w = lambda k, shp: jax.random.normal(k, shp, jnp.float32) * s
        return {'x': jax.random.normal(ks[0], (B, T, D), jnp.float32), 'q_w': w(ks[1], (D, D)), 'q_b': jnp.zeros((D,), jnp.float32), 'k_w': w(ks[2], (D, D)), 'k_b': jnp.zeros((D,), jnp.float32), 'v_w': w(ks[3], (D, D)), 'v_b': jnp.zeros((D,), jnp.float32), 'o_w': w(ks[4], (D, D)), 'o_b': jnp.zeros((D,), jnp.float32), 'ln1_w': jnp.ones((D,), jnp.float32), 'ln1_b': jnp.zeros((D,), jnp.float32), 'ln2_w': jnp.ones((D,), jnp.float32), 'ln2_b': jnp.zeros((D,), jnp.float32), 'dec_w': w(ks[5], (D, H)), 'dec_b': jnp.full((H,), 5.0, jnp.float32), 'f1_w': w(ks[6], (D, FFN)), 'f1_b': jnp.zeros((FFN,), jnp.float32), 'f2_w': w(ks[7], (FFN, D)), 'f2_b': jnp.zeros((D,), jnp.float32)}
    _L0_attn_in = _L0_attn_setup()

    def _L0_ffn_setup():
        import jax, jax.numpy as jnp
        import numpy as np
        NUM_NOD = 6
        MAX_PREV = 5
        NUM_EDGE = 20
        D = 128
        H = 8
        LN_EPS = 1e-06

        def _layernorm(x, g, b):
            mu = jnp.mean(x, axis=-1, keepdims=True)
            var = jnp.mean(jnp.square(x - mu), axis=-1, keepdims=True)
            return (x - mu) * jax.lax.rsqrt(var + LN_EPS) * g + b

        def _mha(q, k, v, wq, wk, wv, wo):
            B, S, d = q.shape
            dh = d // H
            qh = (q @ wq).reshape(B, S, H, dh)
            kh = (k @ wk).reshape(B, S, H, dh)
            vh = (v @ wv).reshape(B, S, H, dh)
            scores = jnp.einsum('bqhd,bkhd->bhqk', qh, kh) / jnp.sqrt(jnp.asarray(dh, q.dtype))
            attn = jax.nn.softmax(scores, axis=-1)
            ctx = jnp.einsum('bhqk,bkhd->bqhd', attn, vh).reshape(B, S, d)
            return ctx @ wo
        key = jax.random.key(seed)
        ks = jax.random.split(key, 12)
        B, S = (8, 128)
        scale = 1.0 / np.sqrt(D)
        return {'inputs': jax.random.normal(ks[0], (B, S, D), jnp.float32), 'ew': jax.random.uniform(ks[1], (NUM_NOD, 3), jnp.float32), 'act_w': jax.random.uniform(ks[2], (NUM_NOD,), jnp.float32), 'We': jax.random.normal(ks[3], (NUM_EDGE, D, D), jnp.float32) * scale, 'be': jnp.zeros((NUM_EDGE, D), jnp.float32), 'Wq': jax.random.normal(ks[4], (NUM_NOD, D, D), jnp.float32) * scale, 'Wk': jax.random.normal(ks[5], (NUM_NOD, D, D), jnp.float32) * scale, 'Wv': jax.random.normal(ks[6], (NUM_NOD, D, D), jnp.float32) * scale, 'Wo': jax.random.normal(ks[7], (NUM_NOD, D, D), jnp.float32) * scale, 'ln_g': jnp.ones((D,), jnp.float32), 'ln_b': jnp.zeros((D,), jnp.float32)}
    _L0_ffn_in = _L0_ffn_setup()
    _L0_c = _w((lambda *s: np.random.randn(*s).astype(np.float32) * 0.05)(16, 128))
    _L0_wmod = _w((lambda *s: np.random.randn(*s).astype(np.float32) * 0.05)(128, 6 * 128) * 128 ** (-0.5))
    _d = {'L0_attn_x': _L0_attn_in['x'], 'L0_attn_q_w': _L0_attn_in['q_w'], 'L0_attn_q_b': _L0_attn_in['q_b'], 'L0_attn_k_w': _L0_attn_in['k_w'], 'L0_attn_k_b': _L0_attn_in['k_b'], 'L0_attn_v_w': _L0_attn_in['v_w'], 'L0_attn_v_b': _L0_attn_in['v_b'], 'L0_attn_o_w': _L0_attn_in['o_w'], 'L0_attn_o_b': _L0_attn_in['o_b'], 'L0_attn_ln1_w': _L0_attn_in['ln1_w'], 'L0_attn_ln1_b': _L0_attn_in['ln1_b'], 'L0_attn_ln2_w': _L0_attn_in['ln2_w'], 'L0_attn_ln2_b': _L0_attn_in['ln2_b'], 'L0_attn_dec_w': _L0_attn_in['dec_w'], 'L0_attn_dec_b': _L0_attn_in['dec_b'], 'L0_attn_f1_w': _L0_attn_in['f1_w'], 'L0_attn_f1_b': _L0_attn_in['f1_b'], 'L0_attn_f2_w': _L0_attn_in['f2_w'], 'L0_attn_f2_b': _L0_attn_in['f2_b'], 'L0_ffn_ew': _L0_ffn_in['ew'], 'L0_ffn_act_w': _L0_ffn_in['act_w'], 'L0_ffn_We': _L0_ffn_in['We'], 'L0_ffn_be': _L0_ffn_in['be'], 'L0_ffn_Wq': _L0_ffn_in['Wq'], 'L0_ffn_Wk': _L0_ffn_in['Wk'], 'L0_ffn_Wv': _L0_ffn_in['Wv'], 'L0_ffn_Wo': _L0_ffn_in['Wo'], 'L0_ffn_ln_g': _L0_ffn_in['ln_g'], 'L0_ffn_ln_b': _L0_ffn_in['ln_b'], 'L0_c': _L0_c, 'L0_wmod': _L0_wmod}
    _x0 = _d['L0_attn_x']
    _d['L0_attn_x'] = jax.random.normal(jax.random.fold_in(jax.random.key(seed), 1), (16, 512, 128), dtype=_x0.dtype)
    del _x0
    return _d

def reference(L0_attn_x, L0_attn_q_w, L0_attn_q_b, L0_attn_k_w, L0_attn_k_b, L0_attn_v_w, L0_attn_v_b, L0_attn_o_w, L0_attn_o_b, L0_attn_ln1_w, L0_attn_ln1_b, L0_attn_ln2_w, L0_attn_ln2_b, L0_attn_dec_w, L0_attn_dec_b, L0_attn_f1_w, L0_attn_f1_b, L0_attn_f2_w, L0_attn_f2_b, L0_ffn_ew, L0_ffn_act_w, L0_ffn_We, L0_ffn_be, L0_ffn_Wq, L0_ffn_Wk, L0_ffn_Wv, L0_ffn_Wo, L0_ffn_ln_g, L0_ffn_ln_b, L0_c, L0_wmod):

    def _L0_attn_ref(x, q_w, q_b, k_w, k_b, v_w, v_b, o_w, o_b, ln1_w, ln1_b, ln2_w, ln2_b, dec_w, dec_b, f1_w, f1_b, f2_w, f2_b):
        import jax, jax.numpy as jnp
        import numpy as np
        B, T, D, H, FFN = (2, 256, 128, 16, 512)
        K = D // H
        EPS = 1e-06
        LN_EPS = 1e-05
        LAM_MIN = 1e-08

        def _ln(x, w, b):
            m = x.mean(-1, keepdims=True)
            v = ((x - m) ** 2).mean(-1, keepdims=True)
            return (x - m) * jax.lax.rsqrt(v + LN_EPS) * w + b

        def _lion(phi_q, phi_k, v, lam):
            b, h, t, kk = phi_q.shape
            kv = v.shape[-1]
            to_t = lambda a: a.transpose(2, 0, 1, 3)
            qt, kt, vt, lt = (to_t(phi_q), to_t(phi_k), to_t(v), to_t(lam))
            S0 = jnp.zeros((b, h, kk, kv), phi_q.dtype)

            def fwd(S, inp):
                q_t, k_t, v_t, l_t = inp
                S = S * l_t[..., None] + k_t[..., None] * v_t[..., None, :]
                return (S, jnp.einsum('bhk,bhkv->bhv', q_t, S))
            _, out_f = jax.lax.scan(fwd, S0, (qt, kt, vt, lt))
            q_shift = jnp.concatenate([qt[:1], qt[:-1]], axis=0)

            def bwd(R, inp):
                qs_t, k_t, v_t, l_t = inp
                R = l_t[..., None] * (k_t[..., None] * v_t[..., None, :] + R)
                return (R, jnp.einsum('bhk,bhkv->bhv', qs_t, R))
            _, out_b = jax.lax.scan(bwd, S0, (q_shift, kt, vt, lt), reverse=True)
            out_b = jnp.concatenate([out_b[1:], jnp.zeros_like(out_b[:1])], axis=0)
            return (out_f + out_b).transpose(1, 2, 0, 3)
        bb, tt, dd = x.shape
        residual = x
        x_n = _ln(x, ln1_w, ln1_b)
        split = lambda y: y.reshape(bb, tt, H, K).transpose(0, 2, 1, 3)
        q = split(x_n @ q_w + q_b)
        k = split(x_n @ k_w + k_b)
        v = split(x_n @ v_w + v_b)
        phi_q = jax.nn.elu(q) + 1.0
        phi_k = jax.nn.elu(k) + 1.0
        lam = jax.nn.sigmoid(x_n @ dec_w + dec_b)
        lam = jnp.maximum(lam, LAM_MIN).transpose(0, 2, 1)
        lam = jnp.broadcast_to(lam[..., None], (bb, H, tt, K))
        v_ext = jnp.concatenate([v, jnp.ones((bb, H, tt, 1), v.dtype)], axis=-1)
        out = _lion(phi_q, phi_k, v_ext, lam)
        num, den = (out[..., :K], jnp.maximum(out[..., K:], EPS))
        attn = (num / den).transpose(0, 2, 1, 3).reshape(bb, tt, dd)
        x = residual + (attn @ o_w + o_b)
        x2 = _ln(x, ln2_w, ln2_b)
        h = jax.nn.gelu(x2 @ f1_w + f1_b, approximate=False)
        return x + (h @ f2_w + f2_b)

    def _L0_ffn_ref(inputs, ew, act_w, We, be, Wq, Wk, Wv, Wo, ln_g, ln_b):
        import jax, jax.numpy as jnp
        import numpy as np
        NUM_NOD = 6
        MAX_PREV = 5
        NUM_EDGE = 20
        D = 128
        H = 8
        LN_EPS = 1e-06

        def _layernorm(x, g, b):
            mu = jnp.mean(x, axis=-1, keepdims=True)
            var = jnp.mean(jnp.square(x - mu), axis=-1, keepdims=True)
            return (x - mu) * jax.lax.rsqrt(var + LN_EPS) * g + b

        def _mha(q, k, v, wq, wk, wv, wo):
            B, S, d = q.shape
            dh = d // H
            qh = (q @ wq).reshape(B, S, H, dh)
            kh = (k @ wk).reshape(B, S, H, dh)
            vh = (v @ wv).reshape(B, S, H, dh)
            scores = jnp.einsum('bqhd,bkhd->bhqk', qh, kh) / jnp.sqrt(jnp.asarray(dh, q.dtype))
            attn = jax.nn.softmax(scores, axis=-1)
            ctx = jnp.einsum('bhqk,bkhd->bqhd', attn, vh).reshape(B, S, d)
            return ctx @ wo
        nodes = {-1: inputs}
        lind = 0
        for c in range(NUM_NOD):
            nsrc = min(c + 1, MAX_PREV)
            snode = c - nsrc
            eq, ek, ev = (lind + nsrc - 1, lind, lind + nsrc // 2)
            in_q, in_k, in_v = (c - 1, snode, snode + nsrc // 2)
            q = ew[c, 0] * (nodes[in_q] @ We[eq] + be[eq])
            k = ew[c, 1] * (nodes[in_k] @ We[ek] + be[ek])
            v = ew[c, 2] * (nodes[in_v] @ We[ev] + be[ev])
            o = _mha(q, k, v, Wq[c], Wk[c], Wv[c], Wo[c])
            nodes[c] = act_w[c] * o + q
            lind += nsrc
        out = nodes[NUM_NOD - 1]
        return _layernorm(out, ln_g, ln_b)
    x = L0_attn_x
    mod = (_silu(L0_c) @ L0_wmod).reshape(L0_c.shape[0], 6, 1, -1)
    sa, ca, ga, sb, cb, gb = (mod[:, 0], mod[:, 1], mod[:, 2], mod[:, 3], mod[:, 4], mod[:, 5])
    ga = (2 * (ga >= 0) - 1) * jnp.maximum(jnp.abs(ga), 0.25)
    gb = (2 * (gb >= 0) - 1) * jnp.maximum(jnp.abs(gb), 0.25)
    h = _layernorm(x, axis=-1) * (1 + ca) + sa
    x = x + ga * _L0_attn_ref(h, L0_attn_q_w, L0_attn_q_b, L0_attn_k_w, L0_attn_k_b, L0_attn_v_w, L0_attn_v_b, L0_attn_o_w, L0_attn_o_b, L0_attn_ln1_w, L0_attn_ln1_b, L0_attn_ln2_w, L0_attn_ln2_b, L0_attn_dec_w, L0_attn_dec_b, L0_attn_f1_w, L0_attn_f1_b, L0_attn_f2_w, L0_attn_f2_b)
    h = _layernorm(x, axis=-1) * (1 + cb) + sb
    x = x + gb * _L0_ffn_ref(h, L0_ffn_ew, L0_ffn_act_w, L0_ffn_We, L0_ffn_be, L0_ffn_Wq, L0_ffn_Wk, L0_ffn_Wv, L0_ffn_Wo, L0_ffn_ln_g, L0_ffn_ln_b)
    return x

_drawn_inputs = setup_inputs


def setup_inputs(seed=0):
    import zlib

    import numpy as np

    out = dict(_drawn_inputs(seed))
    spreads = {'L0_attn_q_b': (0.0, 2.0),
     'L0_attn_k_b': (0.0, 2.0),
     'L0_attn_v_b': (0.0, 0.8),
     'L0_attn_o_b': (0.0, 0.318),
     'L0_attn_ln1_w': (1.0, 0.6),
     'L0_attn_ln1_b': (0.0, 0.8),
     'L0_attn_ln2_w': (1.0, 0.6),
     'L0_attn_ln2_b': (0.0, 0.8),
     'L0_attn_dec_b': (5.0, 0.6),
     'L0_attn_f1_b': (0.0, 0.8),
     'L0_attn_f2_b': (0.0, 0.337),
     'L0_ffn_be': (0.0, 0.1),
     'L0_ffn_ln_g': (1.0, 0.2),
     'L0_ffn_ln_b': (0.0, 0.361)}
    factors = {'L0_attn_q_w': 8.0,
     'L0_attn_k_w': 8.0,
     'L0_attn_v_w': 8.0,
     'L0_attn_o_w': 8.0,
     'L0_attn_dec_w': 8.0,
     'L0_attn_f1_w': 4.263,
     'L0_attn_f2_w': 3.831,
     'L0_ffn_Wq': 200.0,
     'L0_ffn_Wk': 200.0}
    for name, (base, spread) in spreads.items():
        noise = np.random.default_rng([zlib.crc32(name.encode()), seed]).standard_normal(out[name].shape)
        drawn = base * np.exp(spread * noise) if base else spread * noise
        out[name] = jnp.asarray(drawn.astype(out[name].dtype))
    for name, factor in factors.items():
        out[name] = (out[name] * factor).astype(out[name].dtype)
    return out
```

```python
import numpy as np
import concourse.bass as bass
from concourse import mybir
from contextlib import ExitStack

FP32 = mybir.dt.float32
BF16 = mybir.dt.bfloat16
ALU = mybir.AluOpType
ACT = mybir.ActivationFunctionType
AX = mybir.AxisListType

P = 128
B, T, D = 16, 512, 128
CH = T // P

LH, LK = 16, 8
FFN = 512
FC = FFN // P
LION_EPS, LAM_MIN = 1e-6, 1e-8
LW = 2 * LK
LR = LH // 4

NODES, MAX_PREV = 6, 5
MH, DH = 8, 16
MG = MH // 4
PARTS = 6
SROWS = PARTS * DH
K_PART = (0, 0, 1, 1, 0, 2)
Q_PART = (0, 1, 0, 1, 2, 0)


def node_inputs():
    out, first = [], 0
    for c in range(NODES):
        n = min(c + 1, MAX_PREV)
        out.append(((first + n - 1, first, first + n // 2), (c - 1, c - n, c - n + n // 2)))
        first += n
    return out


WIRING = node_inputs()


class Steps:

    def __init__(self, sem, names):
        self.sem, self.names = sem, names
        self.place = {n: i for i, n in enumerate(names)}
        assert len(self.place) == len(names)
        self.next = [0] * len(sem)

    def sig(self, lane, name):
        assert self.names[self.next[lane]] == name, (self.names[self.next[lane]], name)
        self.next[lane] = (self.next[lane] + 1) % len(self.names)
        return self.sem[lane]

    def at(self, name, it):
        return it * len(self.names) + self.place[name] + 2

    def all(self, it):
        return it * len(self.names) + 1

    def start(self, eng):
        for sem in self.sem:
            eng.sem_inc(sem, 1)


def modulation_phase(nc, a, mod_rows):
    ctx = ExitStack()
    with ctx:
        def sb(name, shape, dt=FP32):
            return ctx.enter_context(nc.sbuf_tensor("m_" + name, shape, dt))

        def sem(name):
            return ctx.enter_context(nc.semaphore("m_" + name))

        cT, wmod = sb("cT", [D, B]), sb("wmod", [D, 6 * D])
        ex, one_ex, silu = sb("ex", [D, B]), sb("one_ex", [D, B]), sb("silu", [D, B])
        mod = sb("mod", [B, 6, D])
        sign, size = sb("sign", [B, 2, D]), sb("size", [B, 2, D])
        ps = ctx.enter_context(nc.psum_tensor("m_ps", [P, 2, 512], FP32))
        loaded, exp_done, dve_done, mod_summed, stored = (sem(n) for n in ("loaded", "exp_done", "dve_done", "mod_summed", "stored"))
        gates = mod[:, 2::3, :]
        block = ctx.enter_context(nc.Block())

        @block.sync
        def _(sync):
            sync.dma_start(cT[:], a["c"].rearrange("b d -> d b"), allow_slow_non_contiguous=True).then_inc(loaded, 16)
            sync.dma_start(wmod[:], a["wmod"]).then_inc(loaded, 16)
            sync.wait_ge(dve_done, 11)
            sync.dma_start(mod_rows, mod[:].rearrange("b k n -> b (k n)")).then_inc(stored, 16)
            sync.wait_ge(stored, 16)

        @block.scalar
        def _(ac):
            ac.wait_ge(loaded, 32)
            ac.activation(ex[:], cT[:], ACT.Exp, scale=-1.0).then_inc(exp_done, 1)

        @block.tensor
        def _(pe):
            pe.wait_ge(dve_done, 3)
            for k in range(2):
                ins = pe.matmul(ps[0:B, k, 0:3 * D], silu[:], wmod[:, k * 3 * D:(k + 1) * 3 * D], start=True, stop=True)
            ins.then_inc(mod_summed, 1)

        @block.vector
        def _(ve):
            ve.wait_ge(exp_done, 1)
            ve.tensor_scalar(one_ex[:], ex[:], 1.0, None, ALU.add).then_inc(dve_done, 1)
            ve.wait_ge(dve_done, 1)
            ve.reciprocal(ex[:], one_ex[:]).then_inc(dve_done, 1)
            ve.wait_ge(dve_done, 2)
            ve.tensor_tensor(silu[:], cT[:], ex[:], ALU.mult).then_inc(dve_done, 1)
            ve.wait_ge(mod_summed, 1)
            for k in range(2):
                ve.tensor_copy(mod[:, 3 * k:3 * k + 3, :].rearrange("b k n -> b (k n)"), ps[0:B, k, 0:3 * D]).then_inc(dve_done, 1)
            ve.wait_ge(dve_done, 5)
            for k in (1, 4):
                ve.tensor_scalar(mod[:, k, :], mod[:, k, :], 1.0, None, ALU.add).then_inc(dve_done, 1)
            ve.tensor_scalar(sign[:], gates, 0.0, 2.0, ALU.is_ge, ALU.mult).then_inc(dve_done, 1)
            ve.scalar_tensor_tensor(size[:], gates, -1.0, gates, ALU.mult, ALU.max).then_inc(dve_done, 1)
            ve.wait_ge(dve_done, 9)
            ve.tensor_scalar(size[:], size[:], 0.25, None, ALU.max).then_inc(dve_done, 1)
            ve.wait_ge(dve_done, 10)
            ve.scalar_tensor_tensor(gates, sign[:], -1.0, size[:], ALU.add, ALU.mult).then_inc(dve_done, 1)


def decay_attention_phase(nc, a, mod_rows, x_mid):
    ctx = ExitStack()
    with ctx:
        def sb(name, shape, dt=FP32):
            return ctx.enter_context(nc.sbuf_tensor("a_" + name, shape, dt))

        def sems(name):
            return [ctx.enter_context(nc.semaphore(f"a_{name}{p}")) for p in range(2)]

        ident = sb("ident", [P, P])
        upto = sb("upto", [P, P])
        after = sb("after", [P, P])
        blockmask = sb("blockmask", [P, LH, LW])
        headmask = sb("headmask", [P, LH])
        pick = sb("pick", [96, LH, P], BF16)
        unpick = sb("unpick", [96, LH, P], BF16)
        spare = sb("spare", [P, 1])
        pick1 = sb("pick1", [96, LH])
        denrow = sb("denrow", [P, P])
        floor = sb("floor", [P, 1])
        cols = sb("cols", [P, 6])
        rows = sb("rows", [P, 3, D])
        decb = sb("decb", [P, LH])
        f1b = sb("f1b", [P, FC])
        qw, kw, vw = sb("qw", [P, D]), sb("kw", [P, D]), sb("vw", [P, D])
        decw = sb("decw", [P, LH])
        ow = sb("ow", [P, LR, D])
        f1w = sb("f1w", [P, FFN])
        f2w = sb("f2w", [P, FC, D])

        def two(name, shape, dt=FP32):
            return [sb(f"{name}{p}", shape, dt) for p in range(2)]

        x = two("x", [P, CH, D])
        modb = two("modb", [P, 3, D])
        stats, mv = two("stats", [P, CH, 6]), two("mv", [P, CH, 2])
        var, rstd = two("var", [P, CH, 1]), two("rstd", [P, CH, 1])
        minus_half = sb("minus_half", [P, CH, 1])
        xn, h, hn, hob = (two(n, [P, CH, D]) for n in ("xn", "h", "hn", "hob"))
        xnT = two("xnT", [P, T])
        hidden = two("hidden", [P, FC, T])
        tq, rq, tk, rk = ([hidden[p][:, i, :] for p in range(2)] for i in range(4))
        phiq, phik = two("phiq", [P, T]), two("phik", [P, T])
        zb, ez, lnz, ll = (two(n, [P, CH, LH]) for n in ("zb", "ez", "lnz", "ll"))
        ll3 = two("ll3", [P, CH, 3, 32])
        llrep = two("llrep", [P, CH, LH, LK])
        vaug = two("vaug", [P, CH, LH + 1, LW])
        cum3 = two("cum3", [96, T], BF16)
        cumr = two("cumr", [96, T])
        e1t, e2t = two("e1t", [P, T]), two("e2t", [P, T])
        etok = two("etok", [P, 2, CH, LH])
        attnT = two("attnT", [P, LR, T])
        kf, kb = ([attnT[p][:, i, :].rearrange("p (c h k) -> p c h k", c=CH, h=LH) for p in range(2)] for i in range(2))
        st = two("st", [P, 6, LH, LW])
        stp = two("stp", [P, 6, LR, 4, 32])
        qf, qb = two("qf", [P, T]), two("qb", [P, T])
        qm = two("qm", [P, 2, T])
        absd, dec, at = two("absd", [P, 2, T]), two("dec", [P, 2, T]), two("at", [P, 2, T])
        un, rden = two("un", [P, T]), two("rden", [P, T])
        ps = ctx.enter_context(nc.psum_tensor("a_ps", [P, 8, T], FP32))

        def bank(p, n):
            return ps[:, 4 * p + n, :]

        def chunked(ap):
            return ap.rearrange("p (c n) -> p c n", c=CH)

        ld_const = ctx.enter_context(nc.semaphore("a_const_loaded"))
        picks_ready = ctx.enter_context(nc.semaphore("a_picks_ready"))
        pads_zero = ctx.enter_context(nc.semaphore("a_pads_zero"))
        x_loaded, x_stored = sems("x_loaded"), sems("x_stored")
        heads, rounds = range(LH), range(LR)

        def norm(tag):
            return [tag + s for s in ("stats", "aggr", "eps", "out")]

        V = Steps(sems("vector_steps"), norm("ln1") + norm("ln2") + ["tq", "tk", "zb", "vaug", "ll", "ll3", "llrep",
                  "ct1", "ct2", "ct3", "ct4", "kf", "kb", "s1", "r2", "s2", "s3", "r1", "r0"]
                  + sum([([f"un{i // 4 - 1}"] if i and i % 4 == 0 else []) + [f"at{i}"] + ([f"div{(i - 6) // 4}"] if i >= 6 and i % 4 == 2 else []) for i in heads], [])
                  + [f"un{LR - 1}", f"div{LR - 1}", "x1"] + norm("ln3") + ["y"])
        S = Steps(sems("scalar_steps"), ["xnT", "rq", "rk", "eq", "ek", "ez", "lnz", "e1t", "e2t", "etok"]
                  + sum([[f"abs{i}", f"dec{i}"] for i in heads], [])
                  + ["xn2T"] + [f"gelu{m}" for m in range(FC)])
        G = Steps(sems("gpsimd_steps"), ["ln1rstd", "h1", "h", "ln2rstd", "hob", "phiq", "phik", "qf", "qb", "mask0"]
                  + [f"sp{i}" for i in range(6)]
                  + sum([[f"mask{i}"] + ([f"attn{i // 4 - 2}"] if i >= 8 and i % 4 == 0 else []) for i in heads[1:]], [])
                  + [f"attn{LR - 2}", f"attn{LR - 1}", "ln3rstd", "x1f", "gy", "xo"])
        M = Steps(sems("tensor_steps"), ["tr1", "qT", "kT", "dec", "v", "ct", "ce1", "ce2", "tok", "ktok",
                  "F01", "F2G3", "G12", "diff0", "scores0", "inter0"]
                  + sum([[f"diff{i}", f"scores{i}", f"intra{i - 1}"] + ([f"inter{i // 4}"] if i % 4 == 0 else [])
                         + ([f"den{(i - 6) // 4}"] if i >= 6 and i % 4 == 2 else []) for i in heads[1:]], [])
                  + [f"intra{LH - 1}", f"den{LR - 1}", "oproj", "tr2"] + [f"f1_{m}" for m in range(FC)] + ["f2"])
        N_CONST = 16 * (15 + 6 + 3 + 1 + 4)
        block = ctx.enter_context(nc.Block())

        @block.sync
        def _(sync):
            loads = [
                (ident, a["c_ident"]), (upto, a["c_upto"]), (after, a["c_after"]),
                (blockmask, a["c_blockmask"]), (headmask, a["c_headmask"]), (pick1, a["c_pick"]),
                (denrow, a["c_denrow_a"]), (floor, a["c_floor"]),
                (qw, a["q_w"]), (kw, a["k_w"]), (vw, a["v_w"]), (decw, a["dec_w"]), (f1w, a["f1_w"]),
                (f2w, a["f2_w"].rearrange("(m p) n -> p m n", p=P)),
                (f1b, a["f1_b"].rearrange("(m p) -> p m", p=P)),
            ]
            for dst, src in loads:
                sync.dma_start(dst[:], src, allow_slow_non_contiguous=True).then_inc(ld_const, 16)
            for i, n in enumerate(("ln1_w", "ln1_b", "ln2_w", "ln2_b", "q_b", "k_b")):
                sync.dma_start(cols[:, i:i + 1], a[n].rearrange("(p a) -> p a", a=1)).then_inc(ld_const, 16)
            for i, n in enumerate(("v_b", "o_b", "f2_b")):
                sync.dma_start(rows[:, i, :], a[n].rearrange("(a n) -> a n", a=1).broadcast_to([P, D])).then_inc(ld_const, 16)
            sync.dma_start(decb[:], a["dec_b"].rearrange("(a n) -> a n", a=1).broadcast_to([P, LH])).then_inc(ld_const, 16)
            for steps in (M, V, S, G):
                steps.start(sync)
            for p in range(2):
                sync.sem_inc(x_stored[p], 16)
            sync.wait_ge(pads_zero, 1)
            for g in range(4):
                src = a["o_w"].rearrange("(r g v) n -> g v r n", g=4, v=LK)[g]
                sync.dma_start(ow[32 * g:32 * g + LK, :, :], src).then_inc(ld_const, 16)
            with sync.Fori(0, B // 2) as it:
                for p in range(2):
                    b = it * 2 + p
                    sync.wait_ge(x_stored[p], it * 16 + 16)
                    sync.dma_start(x[p][:], a["x"][bass.ds(b, 1)].rearrange("a (c p) n -> (a p) c n", p=P)).then_inc(x_loaded[p], 16)
                    sync.dma_start(modb[p][:], mod_rows[bass.ds(b, 1), 0:3 * D].rearrange("a (k n) -> a k n", k=3).broadcast_to([P, 3, D])).then_inc(x_loaded[p], 16)
                for p in range(2):
                    b = it * 2 + p
                    sync.wait_ge(G.sem[p], G.at("xo", it))
                    sync.dma_start(x_mid[bass.ds(b, 1)].rearrange("a (c p) n -> (a p) c n", p=P), xn[p][:]).then_inc(x_stored[p], 16)
            for p in range(2):
                sync.wait_ge(x_stored[p], 16 * (B // 2) + 16)

        @block.gpsimd
        def _(gp):
            def inverse_root(it, p, tag):
                gp.wait_ge(V.sem[p], V.at(tag + "eps", it))
                gp.tensor_tensor(rstd[p][:], var[p][:], minus_half[:], ALU.pow).then_inc(G.sig(p, tag + "rstd"), 1)

            def s_rstd1(it, p):
                inverse_root(it, p, "ln1")

            def s_h(it, p):
                gp.wait_ge(x_loaded[p], it * 32 + 32)
                gp.wait_ge(V.sem[p], V.at("ln1out", it))
                gp.tensor_tensor(xn[p][:], xn[p][:], modb[p][:, 1:2, :].broadcast_to([P, CH, D]), ALU.mult).then_inc(G.sig(p, "h1"), 1)
                gp.wait_ge(G.sem[p], G.at("h1", it))
                gp.tensor_tensor(h[p][:], xn[p][:], modb[p][:, 0:1, :].broadcast_to([P, CH, D]), ALU.add).then_inc(G.sig(p, "h"), 1)

            def s_hob(it, p):
                inverse_root(it, p, "ln2")
                gp.tensor_tensor(hob[p][:], h[p][:], rows[:, 1:2, :].broadcast_to([P, CH, D]), ALU.add).then_inc(G.sig(p, "hob"), 1)

            def s_phi(it, p):
                gp.wait_ge(S.sem[p], S.at("eq", it))
                gp.tensor_tensor(phiq[p][:], rq[p], tq[p], ALU.add).then_inc(G.sig(p, "phiq"), 1)
                gp.wait_ge(S.sem[p], S.at("ek", it))
                gp.tensor_tensor(phik[p][:], rk[p], tk[p], ALU.add).then_inc(G.sig(p, "phik"), 1)

            def s_q(it, p):
                gp.wait_ge(G.sem[p], G.at("phiq", it))
                gp.wait_ge(S.sem[p], S.at("e2t", it))
                gp.tensor_tensor(qf[p][:], phiq[p][:], e1t[p][:], ALU.mult).then_inc(G.sig(p, "qf"), 1)
                gp.tensor_tensor(qb[p][:], phiq[p][:], e2t[p][:], ALU.mult).then_inc(G.sig(p, "qb"), 1)

            def s_mask(i):
                def go(it, p):
                    if i >= 2:
                        gp.wait_ge(M.sem[p], M.at(f"scores{i - 2}", it))
                    gp.tensor_tensor(qm[p][:, i % 2, :], phiq[p][:], headmask[:, i:i + 1].broadcast_to([P, T]), ALU.mult).then_inc(G.sig(p, f"mask{i}"), 1)
                return go

            def s_states(it, p):
                for i, name in enumerate(("s1", "s2", "s3", "r0", "r1", "r2")):
                    gp.wait_ge(V.sem[p], V.at(name, it))
                    gp.tensor_tensor(stp[p][:, i].rearrange("p r g w -> p (r g) w")[:, :, 0:LW], st[p][:, i], blockmask[:], ALU.mult).then_inc(G.sig(p, f"sp{i}"), 1)

            def s_attn(r):
                def go(it, p):
                    gp.wait_ge(V.sem[p], V.at(f"div{r}", it))
                    gp.tensor_tensor(attnT[p][:, r, :], un[p][:], rden[p][:], ALU.mult).then_inc(G.sig(p, f"attn{r}"), 1)
                return go

            def s_x1f(it, p):
                inverse_root(it, p, "ln3")
                gp.tensor_tensor(hob[p][:], h[p][:], rows[:, 2:3, :].broadcast_to([P, CH, D]), ALU.add).then_inc(G.sig(p, "x1f"), 1)

            def s_out(it, p):
                gp.wait_ge(V.sem[p], V.at("y", it))
                gp.tensor_tensor(hn[p][:], hn[p][:], modb[p][:, 2:3, :].broadcast_to([P, CH, D]), ALU.mult).then_inc(G.sig(p, "gy"), 1)
                gp.wait_ge(G.sem[p], G.at("gy", it))
                gp.tensor_tensor(xn[p][:], hn[p][:], x[p][:], ALU.add).then_inc(G.sig(p, "xo"), 1)

            for p in range(2):
                gp.memset(ll3[p][:], 0.0)
                gp.memset(stp[p][:], 0.0)
                gp.memset(vaug[p][:, :, 0:LH, :], 1.0)
                gp.memset(vaug[p][:, :, LH:LH + 1, :], 0.0)
            gp.memset(minus_half[:], -0.5)
            gp.memset(ow[:], 0.0).then_inc(pads_zero, 1)
            gp.wait_ge(ld_const, N_CONST)
            masks = sum([[s_mask(i)] + ([s_attn(i // 4 - 2)] if i >= 8 and i % 4 == 0 else []) for i in heads[1:]], [])
            with gp.Fori(0, B // 2) as it:
                for stage in [s_rstd1, s_h, s_hob, s_phi, s_q, s_mask(0), s_states] + masks + [s_attn(LR - 2), s_attn(LR - 1), s_x1f, s_out]:
                    for p in range(2):
                        stage(it, p)

        @block.vector
        def _(ve):
            def norm_steps(it, p, tag, src, dst, eps):
                for c in range(CH):
                    ins = ve.bn_stats(stats[p][:, c, :], src[:, c, :])
                ins.then_inc(V.sig(p, tag + "stats"), 1)
                ve.wait_ge(V.sem[p], V.at(tag + "stats", it))
                ve.memset(spare[:], 0.0)
                for c in range(CH):
                    ins = ve.bn_aggr(mv[p][:, c, :], stats[p][:, c, :])
                ins.then_inc(V.sig(p, tag + "aggr"), 1)
                ve.wait_ge(V.sem[p], V.at(tag + "aggr", it))
                ve.tensor_scalar(var[p][:], mv[p][:, :, 1:2], eps, None, ALU.add).then_inc(V.sig(p, tag + "eps"), 1)
                ve.wait_ge(G.sem[p], G.at(tag + "rstd", it))
                for c in range(CH):
                    ins = ve.tensor_scalar(dst[:, c, :], src[:, c, :], mv[p][:, c, 0:1], rstd[p][:, c, :], ALU.subtract, ALU.mult)
                ins.then_inc(V.sig(p, tag + "out"), 1)

            def s_ln1(it, p):
                ve.wait_ge(x_loaded[p], it * 32 + 32)
                ve.wait_ge(x_stored[p], it * 16 + 16)
                norm_steps(it, p, "ln1", x[p], xn[p], 1e-5)

            def s_ln2(it, p):
                ve.wait_ge(G.sem[p], G.at("h", it))
                norm_steps(it, p, "ln2", h[p], hn[p], 1e-5)

            def s_qk(it, p):
                ve.wait_ge(M.sem[p], M.at("qT", it))
                ve.tensor_scalar(tq[p], bank(p, 1), cols[:, 4:5], 0.0, ALU.add, ALU.min).then_inc(V.sig(p, "tq"), 1)
                ve.wait_ge(M.sem[p], M.at("kT", it))
                ve.tensor_scalar(tk[p], bank(p, 2), cols[:, 5:6], 0.0, ALU.add, ALU.min).then_inc(V.sig(p, "tk"), 1)
                ve.wait_ge(M.sem[p], M.at("dec", it))
                ve.tensor_tensor(zb[p][:], bank(p, 3)[:, 0:CH * LH].rearrange("p (c h) -> p c h", c=CH),
                                 decb[:].rearrange("p (a h) -> p a h", a=1).broadcast_to([P, CH, LH]), ALU.add).then_inc(V.sig(p, "zb"), 1)
                ve.wait_ge(M.sem[p], M.at("v", it))
                ve.tensor_tensor(vaug[p][:, :, 0:LH, 0:LK], bank(p, 0).rearrange("p (c h v) -> p c h v", c=CH, h=LH),
                                 rows[:, 0:1, :].rearrange("p a (h v) -> p a h v", h=LH).broadcast_to([P, CH, LH, LK]), ALU.add).then_inc(V.sig(p, "vaug"), 1)

            def s_ll(it, p):
                ve.wait_ge(S.sem[p], S.at("lnz", it))
                ve.tensor_scalar(ll[p][:], lnz[p][:], -1.0, float(np.log(LAM_MIN)), ALU.mult, ALU.max).then_inc(V.sig(p, "ll"), 1)
                ve.wait_ge(V.sem[p], V.at("ll", it))
                ve.tensor_copy(ll3[p][:, :, :, 0:LH], ll[p][:].rearrange("p c (a h) -> p c a h", a=1).broadcast_to([P, CH, 3, LH])).then_inc(V.sig(p, "ll3"), 1)
                ve.tensor_copy(llrep[p][:], ll[p][:].rearrange("p c (h a) -> p c h a", a=1).broadcast_to([P, CH, LH, LK])).then_inc(V.sig(p, "llrep"), 1)

            def s_cum(it, p):
                ve.wait_ge(M.sem[p], M.at("ct", it))
                ve.tensor_copy(cum3[p][:], bank(p, 3)[0:96, :]).then_inc(V.sig(p, "ct1"), 1)
                ve.wait_ge(V.sem[p], V.at("ct1", it))
                ve.tensor_tensor(cumr[p][:], bank(p, 3)[0:96, :], cum3[p][:], ALU.subtract).then_inc(V.sig(p, "ct2"), 1)
                ve.wait_ge(V.sem[p], V.at("ct2", it))
                ve.tensor_copy(cum3[p][32:64, :], cumr[p][32:64, :])
                ve.tensor_copy(cum3[p][64:96, :], cumr[p][64:96, :]).then_inc(V.sig(p, "ct3"), 1)
                ve.wait_ge(V.sem[p], V.at("ct3", it))
                ve.tensor_tensor(cum3[p][64:96, :], cumr[p][64:96, :], cum3[p][64:96, :], ALU.subtract).then_inc(V.sig(p, "ct4"), 1)

            def s_ktok(it, p):
                ve.wait_ge(M.sem[p], M.at("ktok", it))
                ve.wait_ge(S.sem[p], S.at("etok", it))
                keys = bank(p, 3).rearrange("p (ch k) -> p ch k", k=LK)
                for i, (dst, name) in enumerate(((kf[p], "kf"), (kb[p], "kb"))):
                    fade = etok[p][:, 1 - i].rearrange("p c (h a) -> p (c h) a", a=1).broadcast_to([P, CH * LH, LK])
                    ve.tensor_tensor(dst.rearrange("p c h k -> p (c h) k"), keys, fade, ALU.mult).then_inc(V.sig(p, name), 1)

            def s_states(it, p):
                def flat(ap):
                    return ap.rearrange("p h w -> p (h w)")
                half = LH * LW
                e = [e1t[p][:, c * P + P - 1:c * P + P] for c in range(CH)]
                ve.wait_ge(M.sem[p], M.at("F01", it))
                ve.tensor_copy(flat(st[p][:, 0]), bank(p, 0)[:, 0:half]).then_inc(V.sig(p, "s1"), 1)
                ve.wait_ge(M.sem[p], M.at("F2G3", it))
                ve.tensor_copy(flat(st[p][:, 5]), bank(p, 1)[:, half:2 * half]).then_inc(V.sig(p, "r2"), 1)
                ve.wait_ge(V.sem[p], V.at("s1", it))
                ve.scalar_tensor_tensor(flat(st[p][:, 1]), flat(st[p][:, 0]), e[1], bank(p, 0)[:, half:2 * half], ALU.mult, ALU.add).then_inc(V.sig(p, "s2"), 1)
                ve.wait_ge(V.sem[p], V.at("s2", it))
                ve.scalar_tensor_tensor(flat(st[p][:, 2]), flat(st[p][:, 1]), e[2], bank(p, 1)[:, 0:half], ALU.mult, ALU.add).then_inc(V.sig(p, "s3"), 1)
                ve.wait_ge(M.sem[p], M.at("G12", it))
                ve.scalar_tensor_tensor(flat(st[p][:, 4]), flat(st[p][:, 5]), e[2], bank(p, 2)[:, half:2 * half], ALU.mult, ALU.add).then_inc(V.sig(p, "r1"), 1)
                ve.wait_ge(V.sem[p], V.at("r1", it))
                ve.scalar_tensor_tensor(flat(st[p][:, 3]), flat(st[p][:, 4]), e[1], bank(p, 2)[:, 0:half], ALU.mult, ALU.add).then_inc(V.sig(p, "r0"), 1)

            def s_at(i):
                def go(it, p):
                    ve.wait_ge(M.sem[p], M.at(f"scores{i}", it))
                    ve.wait_ge(S.sem[p], S.at(f"dec{i}", it))
                    if i >= 2:
                        ve.wait_ge(M.sem[p], M.at(f"intra{i - 2}", it))
                    ve.tensor_tensor(at[p][:, i % 2, :], bank(p, 0), dec[p][:, i % 2, :], ALU.mult).then_inc(V.sig(p, f"at{i}"), 1)
                return go

            def s_un(r):
                def go(it, p):
                    ve.wait_ge(M.sem[p], M.at(f"intra{4 * r + 3}", it))
                    if r:
                        ve.wait_ge(M.sem[p], M.at(f"den{r - 1}", it))
                        ve.wait_ge(G.sem[p], G.at(f"attn{r - 1}", it))
                    ve.tensor_scalar(un[p][:], bank(p, 1), floor[:], None, ALU.max).then_inc(V.sig(p, f"un{r}"), 1)
                return go

            def s_div(r):
                def go(it, p):
                    ve.wait_ge(M.sem[p], M.at(f"den{r}", it))
                    if r:
                        ve.wait_ge(G.sem[p], G.at(f"attn{r - 1}", it))
                    ve.reciprocal(rden[p][:], bank(p, 2)).then_inc(V.sig(p, f"div{r}"), 1)
                return go

            def s_x1(it, p):
                ve.wait_ge(M.sem[p], M.at("oproj", it))
                ve.wait_ge(G.sem[p], G.at("hob", it))
                ve.tensor_tensor(h[p][:], chunked(bank(p, 0)), hob[p][:], ALU.add).then_inc(V.sig(p, "x1"), 1)
                ve.wait_ge(V.sem[p], V.at("x1", it))
                norm_steps(it, p, "ln3", h[p], hn[p], 1e-5)

            def s_y(it, p):
                ve.wait_ge(M.sem[p], M.at("f2", it))
                ve.wait_ge(G.sem[p], G.at("x1f", it))
                ve.tensor_tensor(hn[p][:], chunked(bank(p, 2)), hob[p][:], ALU.add).then_inc(V.sig(p, "y"), 1)

            ve.wait_ge(ld_const, N_CONST)
            ve.wait_ge(pads_zero, 1)
            spread = pick1[:].rearrange("p (h a) -> p h a", a=1).broadcast_to([96, LH, P])
            ve.tensor_copy(pick[:], spread).then_inc(picks_ready, 1)
            ve.wait_ge(picks_ready, 1)
            ve.tensor_scalar(unpick[:], pick[:], -1.0, None, ALU.mult).then_inc(picks_ready, 1)
            attn = sum([([s_un(i // 4 - 1)] if i and i % 4 == 0 else []) + [s_at(i)] + ([s_div((i - 6) // 4)] if i >= 6 and i % 4 == 2 else []) for i in heads], [])
            with ve.Fori(0, B // 2) as it:
                for stage in [s_ln1, s_ln2, s_qk, s_ll, s_cum, s_ktok, s_states] + attn + [s_un(LR - 1), s_div(LR - 1), s_x1, s_y]:
                    for p in range(2):
                        stage(it, p)

        @block.scalar
        def _(ac):
            def s_xnT(it, p):
                ac.wait_ge(M.sem[p], M.at("tr1", it))
                ac.activation(xnT[p][:], bank(p, 0), ACT.Identity, bias=cols[:, 1:2], scale=cols[:, 0:1]).then_inc(S.sig(p, "xnT"), 1)

            def s_phi(it, p):
                ac.wait_ge(M.sem[p], M.at("kT", it))
                ac.wait_ge(V.sem[p], V.at("tq", it))
                ac.activation(rq[p], bank(p, 1), ACT.Relu, bias=cols[:, 4:5]).then_inc(S.sig(p, "rq"), 1)
                ac.wait_ge(V.sem[p], V.at("tk", it))
                ac.activation(rk[p], bank(p, 2), ACT.Relu, bias=cols[:, 5:6]).then_inc(S.sig(p, "rk"), 1)
                ac.activation(tq[p], tq[p], ACT.Exp).then_inc(S.sig(p, "eq"), 1)
                ac.activation(tk[p], tk[p], ACT.Exp).then_inc(S.sig(p, "ek"), 1)

            def s_decay(it, p):
                ac.wait_ge(V.sem[p], V.at("zb", it))
                ac.activation(ez[p][:], zb[p][:], ACT.Exp, scale=-1.0).then_inc(S.sig(p, "ez"), 1)
                ac.wait_ge(S.sem[p], S.at("ez", it))
                ac.activation(lnz[p][:], ez[p][:], ACT.Ln, bias=1.0).then_inc(S.sig(p, "lnz"), 1)

            def s_fades(it, p):
                ac.wait_ge(M.sem[p], M.at("ce1", it))
                ac.activation(e1t[p][:], bank(p, 0), ACT.Exp).then_inc(S.sig(p, "e1t"), 1)
                ac.wait_ge(M.sem[p], M.at("ce2", it))
                ac.activation(e2t[p][:], bank(p, 1), ACT.Exp).then_inc(S.sig(p, "e2t"), 1)
                ac.wait_ge(M.sem[p], M.at("tok", it))
                ac.activation(etok[p][:].rearrange("p a c h -> p (a c h)"), bank(p, 2)[:, 0:2 * CH * LH], ACT.Exp).then_inc(S.sig(p, "etok"), 1)

            def s_head(i):
                def go(it, p):
                    ac.wait_ge(M.sem[p], M.at(f"diff{i}", it))
                    ac.activation(absd[p][:, i % 2, :], bank(p, 3), ACT.Abs).then_inc(S.sig(p, f"abs{i}"), 1)
                    ac.wait_ge(S.sem[p], S.at(f"abs{i}", it))
                    if i >= 2:
                        ac.wait_ge(V.sem[p], V.at(f"at{i - 2}", it))
                    ac.activation(dec[p][:, i % 2, :], absd[p][:, i % 2, :], ACT.Exp, scale=-1.0).then_inc(S.sig(p, f"dec{i}"), 1)
                return go

            def s_xn2T(it, p):
                ac.wait_ge(M.sem[p], M.at("tr2", it))
                ac.activation(xnT[p][:], bank(p, 1), ACT.Identity, bias=cols[:, 3:4], scale=cols[:, 2:3]).then_inc(S.sig(p, "xn2T"), 1)

            def s_gelu(it, p):
                for m in range(FC):
                    ac.wait_ge(M.sem[p], M.at(f"f1_{m}", it))
                    ac.activation(hidden[p][:, m, :], bank(p, (2 + m) % 4), ACT.Gelu, bias=f1b[:, m:m + 1]).then_inc(S.sig(p, f"gelu{m}"), 1)

            ac.wait_ge(ld_const, N_CONST)
            attn = [s_head(i) for i in heads]
            with ac.Fori(0, B // 2) as it:
                for stage in [s_xnT, s_phi, s_decay, s_fades] + attn + [s_xn2T, s_gelu]:
                    for p in range(2):
                        stage(it, p)

        @block.tensor
        def _(pe):
            def transposes(dst, src):
                for c in range(CH):
                    ins = pe.transpose(dst[:, c * P:(c + 1) * P], src[:, c * P:(c + 1) * P], ident[:])
                return ins

            def s_tr1(it, p):
                pe.wait_ge(S.sem[p], S.all(it))
                pe.wait_ge(V.sem[p], V.at("ln2out", it))
                transposes(bank(p, 0), hn[p][:].rearrange("p c n -> p (c n)")).then_inc(M.sig(p, "tr1"), 1)

            def s_proj(it, p):
                pe.wait_ge(S.sem[p], S.at("xnT", it))
                pe.matmul(bank(p, 1), qw[:], xnT[p][:], start=True, stop=True).then_inc(M.sig(p, "qT"), 1)
                pe.matmul(bank(p, 2), kw[:], xnT[p][:], start=True, stop=True).then_inc(M.sig(p, "kT"), 1)
                for c in range(CH):
                    ins = pe.matmul(bank(p, 3)[:, c * LH:(c + 1) * LH], xnT[p][:, c * P:(c + 1) * P], decw[:], start=True, stop=True)
                ins.then_inc(M.sig(p, "dec"), 1)
                for c in range(CH):
                    ins = pe.matmul(bank(p, 0)[:, c * D:(c + 1) * D], xnT[p][:, c * P:(c + 1) * P], vw[:], start=True, stop=True)
                ins.then_inc(M.sig(p, "v"), 1)

            def s_cum(it, p):
                pe.wait_ge(V.sem[p], V.at("ll3", it))
                for c in range(CH):
                    ins = pe.matmul(bank(p, 3)[0:96, c * P:(c + 1) * P], ll3[p][:, c].rearrange("p a h -> p (a h)"), upto[:], start=True, stop=True)
                ins.then_inc(M.sig(p, "ct"), 1)
                pe.wait_ge(V.sem[p], V.at("llrep", it))
                for n, tri, name in ((0, upto, "ce1"), (1, after, "ce2")):
                    if n == 1:
                        pe.wait_ge(S.sem[p], S.at("rk", it))
                    for c in range(CH):
                        ins = pe.matmul(bank(p, n)[:, c * P:(c + 1) * P], llrep[p][:, c].rearrange("p h k -> p (h k)"), tri[:], start=True, stop=True)
                    ins.then_inc(M.sig(p, name), 1)
                for n, tri in ((0, upto), (1, after)):
                    ins = pe.matmul(bank(p, 2)[:, n * CH * LH:(n + 1) * CH * LH], tri[:], ll[p][:].rearrange("p c h -> p (c h)"), start=True, stop=True)
                ins.then_inc(M.sig(p, "tok"), 1)

            def s_ktok(it, p):
                pe.wait_ge(V.sem[p], V.at("ct4", it))
                pe.wait_ge(G.sem[p], G.at("phik", it))
                transposes(bank(p, 3), phik[p][:]).then_inc(M.sig(p, "ktok"), 1)

            def s_sums(it, p):
                half = LH * LW

                def one(dst, keys, c):
                    return pe.matmul(dst, keys[:, c].rearrange("p h k -> p (h k)"),
                                     vaug[p][:, c, 0:LH, :].rearrange("p h w -> p (h w)"), start=True, stop=True)
                pe.wait_ge(V.sem[p], V.at("kb", it))
                pe.wait_ge(S.sem[p], S.at("etok", it))
                one(bank(p, 0)[:, 0:half], kf[p], 0)
                one(bank(p, 0)[:, half:2 * half], kf[p], 1).then_inc(M.sig(p, "F01"), 1)
                one(bank(p, 1)[:, 0:half], kf[p], 2)
                one(bank(p, 1)[:, half:2 * half], kb[p], 3).then_inc(M.sig(p, "F2G3"), 1)
                one(bank(p, 2)[:, 0:half], kb[p], 1)
                one(bank(p, 2)[:, half:2 * half], kb[p], 2).then_inc(M.sig(p, "G12"), 1)

            def diff_scores(it, p, i):
                pe.wait_ge(S.sem[p], S.at(f"abs{i - 1}" if i else "etok", it))
                for c in range(CH):
                    cs = slice(c * P, (c + 1) * P)
                    pe.matmul(bank(p, 3)[:, cs], pick[:, i, :], cum3[p][:, cs], start=True, stop=False, skip_group_check=True)
                    ins = pe.matmul(bank(p, 3)[:, cs], cum3[p][:, cs], unpick[:, i, :], start=False, stop=True, skip_group_check=True)
                ins.then_inc(M.sig(p, f"diff{i}"), 1)
                pe.wait_ge(V.sem[p], V.at(f"at{i - 1}" if i else "r0", it))
                pe.wait_ge(G.sem[p], G.at(f"mask{i}", it))
                for c in range(CH):
                    cs = slice(c * P, (c + 1) * P)
                    ins = pe.matmul(bank(p, 0)[:, cs], phik[p][:, cs], qm[p][:, i % 2, cs], start=True, stop=True)
                ins.then_inc(M.sig(p, f"scores{i}"), 1)

            def inter(it, p, r):
                pe.wait_ge(G.sem[p], G.at("sp5", it))
                if r:
                    pe.wait_ge(V.sem[p], V.at(f"un{r - 1}", it))
                first = True
                for c in range(CH):
                    cs = slice(c * P, (c + 1) * P)
                    for n, q in ([(c - 1, qf[p])] if c else []) + ([(3 + c, qb[p])] if c < CH - 1 else []):
                        ins = pe.matmul(bank(p, 1)[:, cs], stp[p][:, n, r].rearrange("p g w -> p (g w)"), q[:, cs],
                                        start=first, stop=False, skip_group_check=True)
                        first = False
                ins.then_inc(M.sig(p, f"inter{r}"), 1)

            def intra(it, p, i):
                g = i % 4
                pe.wait_ge(V.sem[p], V.at(f"at{i}", it))
                for c in range(CH):
                    cs = slice(c * P, (c + 1) * P)
                    ins = pe.matmul(bank(p, 1)[32 * g:32 * g + 32, cs], vaug[p][:, c, i:i + 2, :].rearrange("p h w -> p (h w)"),
                                    at[p][:, i % 2, cs], start=False, stop=True, skip_group_check=True)
                ins.then_inc(M.sig(p, f"intra{i}"), 1)

            def den(it, p, r):
                pe.wait_ge(V.sem[p], V.at(f"un{r}", it))
                pe.wait_ge(V.sem[p], V.at(f"div{r - 1}" if r else "r0", it))
                pe.matmul(bank(p, 2), denrow[:], un[p][:], start=True, stop=True).then_inc(M.sig(p, f"den{r}"), 1)

            def s_first(it, p):
                pe.wait_ge(V.sem[p], V.at("r0", it))
                diff_scores(it, p, 0)
                inter(it, p, 0)

            def s_head(i):
                def go(it, p):
                    diff_scores(it, p, i)
                    intra(it, p, i - 1)
                    if i % 4 == 0:
                        inter(it, p, i // 4)
                    if i >= 6 and i % 4 == 2:
                        den(it, p, (i - 6) // 4)
                return go

            def s_last(it, p):
                intra(it, p, LH - 1)

            def s_lastden(it, p):
                den(it, p, LR - 1)

            def s_oproj(it, p):
                pe.wait_ge(G.sem[p], G.at(f"attn{LR - 1}", it))
                for c in range(CH):
                    for r in rounds:
                        ins = pe.matmul(bank(p, 0)[:, c * D:(c + 1) * D], attnT[p][:, r, c * P:(c + 1) * P], ow[:, r, :],
                                        start=(r == 0), stop=(r == LR - 1))
                ins.then_inc(M.sig(p, "oproj"), 1)

            def s_tr2(it, p):
                pe.wait_ge(V.sem[p], V.at("ln3out", it))
                transposes(bank(p, 1), hn[p][:].rearrange("p c n -> p (c n)")).then_inc(M.sig(p, "tr2"), 1)

            def s_f1(it, p):
                pe.wait_ge(S.sem[p], S.at("xn2T", it))
                for m in range(FC):
                    pe.matmul(bank(p, (2 + m) % 4), f1w[:, m * P:(m + 1) * P], xnT[p][:], start=True, stop=True).then_inc(M.sig(p, f"f1_{m}"), 1)

            def s_f2(it, p):
                pe.wait_ge(S.sem[p], S.at(f"gelu{FC - 1}", it))
                for c in range(CH):
                    for m in range(FC):
                        ins = pe.matmul(bank(p, 2)[:, c * D:(c + 1) * D], hidden[p][:, m, c * P:(c + 1) * P], f2w[:, m, :],
                                        start=(m == 0), stop=(m == FC - 1))
                ins.then_inc(M.sig(p, "f2"), 1)

            pe.wait_ge(ld_const, N_CONST)
            pe.wait_ge(picks_ready, 2)
            with pe.Fori(0, B // 2) as it:
                for stage in ([s_tr1, s_proj, s_cum, s_ktok, s_sums, s_first] + [s_head(i) for i in heads[1:]]
                              + [s_last, s_lastden, s_oproj, s_tr2, s_f1, s_f2]):
                    for p in range(2):
                        stage(it, p)


class Count:

    AHEAD = 4

    def __init__(self, sem, events, slots, by=1):
        self.sem, self.events, self.slots, self.by = sem, events, slots, by

    def start(self, eng):
        eng.sem_inc(self.sem, self.AHEAD * self.events * self.by)

    def at(self, it, s, k=0):
        return it * (self.slots * self.events * self.by) + ((s + self.AHEAD) * self.events + k + 1) * self.by


def chain_weights(nc, a, w):
    ctx = ExitStack()
    with ctx:
        def sb(name, shape, dt=FP32):
            return ctx.enter_context(nc.sbuf_tensor("w_" + name, shape, dt))

        ident = sb("ident", [P, P])
        ew, aw = sb("ew", [P, NODES, 3]), sb("aw", [P, NODES])
        beT = sb("beT", [P, 20])
        edge = sb("edge", [P, 2, NODES, D])
        edgeT = sb("edgeT", [P, 2, NODES, D])
        wkv = sb("wkv", [P, 2, NODES, D])
        wo = sb("wo", [P, NODES, D])
        edge_q = sb("wq", [P, NODES, D])
        wkd = sb("wkd", [P, NODES, D])
        bv = sb("bv", [P, NODES])
        ps = ctx.enter_context(nc.psum_tensor("w_ps", [P, 8, 512], FP32))
        loaded = ctx.enter_context(nc.semaphore("w_loaded"))
        sem = [[ctx.enter_context(nc.semaphore("w_" + n))] for n in ("tensor_steps", "vector_steps")]
        M = Steps(sem[0], ["turned", "joined", "biases", "bo"])
        V = Steps(sem[1], ["ordered", "turned", "joined", "biases", "wo", "bo"])
        block = ctx.enter_context(nc.Block())
        n_loads = [0]

        @block.sync
        def _(sync):
            def load(dst, src):
                n_loads[0] += 16
                sync.dma_start(dst, src, allow_slow_non_contiguous=True).then_inc(loaded, 16)

            load(ident[:], a["c_ident"])
            load(beT[:], a["be"].rearrange("e d -> d e"))
            load(ew[:], a["ew"].rearrange("(x c) k -> x c k", x=1).broadcast_to([P, NODES, 3]))
            load(aw[:], a["act_w"].rearrange("(x c) -> x c", x=1).broadcast_to([P, NODES]))
            load(edge_q[:], a["Wq"].rearrange("c m n -> m c n"))
            load(wkv[:, 0], a["Wk"].rearrange("c m n -> m c n"))
            load(wkv[:, 1], a["Wv"].rearrange("c m n -> m c n"))
            load(wo[:], a["Wo"].rearrange("c m n -> m c n"))
            for c, (edges, _) in enumerate(WIRING):
                load(w["wqe"][:, c, :], a["We"][edges[0]])
                load(edge[:, 0, c, :], a["We"][edges[1]])
                load(edge[:, 1, c, :], a["We"][edges[2]])
            M.start(sync)
            V.start(sync)
            sync.wait_ge(loaded, n_loads[0])

        ALL = 16 * (8 + 3 * NODES)

        @block.tensor
        def _(pe):
            pe.wait_ge(loaded, ALL)
            for k in range(2):
                for c in range(NODES):
                    n = k * NODES + c
                    ins = pe.transpose(ps[:, n // 4, (n % 4) * P:(n % 4 + 1) * P], edge[:, k, c, :], ident[:])
            ins.then_inc(M.sig(0, "turned"), 1)
            pe.wait_ge(V.sem[0], V.at("turned", 0))
            heads = [wkd[:], wkv[:, 1]]
            for k in range(2):
                for c in range(NODES):
                    n = k * NODES + c
                    ins = pe.matmul(ps[:, 3 + n // 4, (n % 4) * P:(n % 4 + 1) * P], edgeT[:, k, c, :], heads[k][:, c, :], start=True, stop=True)
            ins.then_inc(M.sig(0, "joined"), 1)
            for k in range(2):
                for c, (edges, _) in enumerate(WIRING):
                    e = edges[1 + k]
                    ins = pe.matmul(ps[:, 6, k * NODES + c:k * NODES + c + 1], heads[k][:, c, :], beT[:, e:e + 1], start=True, stop=True)
            ins.then_inc(M.sig(0, "biases"), 1)
            pe.wait_ge(V.sem[0], V.at("wo", 0))
            for c in range(NODES):
                ins = pe.matmul(ps[:, 7, c:c + 1], w["wo"][:, c, :], bv[:, c:c + 1], start=True, stop=True)
            ins.then_inc(M.sig(0, "bo"), 1)

        @block.vector
        def _(ve):
            ve.wait_ge(loaded, ALL)
            for c in range(NODES):
                for dst, src in ((w["wq"], edge_q), (wkd, wkv[:, 0])):
                    ins = ve.tensor_copy(dst[:, c, :].rearrange("p (d h) -> p d h", h=MH), src[:, c, :].rearrange("p (h d) -> p d h", h=MH))
            ins.then_inc(V.sig(0, "ordered"), 1)
            ve.wait_ge(M.sem[0], M.at("turned", 0))
            ve.tensor_copy(edgeT[:].rearrange("p k c n -> p (k c n)"), ps[:, 0:3, :].rearrange("p a n -> p (a n)")).then_inc(V.sig(0, "turned"), 1)
            ve.wait_ge(M.sem[0], M.at("joined", 0))
            for k in range(2):
                for c in range(NODES):
                    n = k * NODES + c
                    ins = ve.tensor_scalar((w["wk"], w["wv"])[k][:, c, :], ps[:, 3 + n // 4, (n % 4) * P:(n % 4 + 1) * P],
                                           ew[:, c, 1 + k:2 + k], None, ALU.mult)
            ins.then_inc(V.sig(0, "joined"), 1)
            ve.wait_ge(M.sem[0], M.at("biases", 0))
            ve.tensor_tensor(w["bk"][:], ps[:, 6, 0:NODES], ew[:, :, 1], ALU.mult)
            for c, (edges, _) in enumerate(WIRING):
                ve.tensor_scalar(w["bq"][:, c:c + 1], beT[:, edges[0]:edges[0] + 1], ew[:, c, 0:1], None, ALU.mult)
                ve.tensor_copy(w["eq"][:, c:c + 1], ew[:, c, 0:1])
            ve.tensor_tensor(bv[:], ps[:, 6, NODES:2 * NODES], ew[:, :, 2], ALU.mult).then_inc(V.sig(0, "biases"), 1)
            for c in range(NODES):
                ins = ve.tensor_scalar(w["wo"][:, c, :], wo[:, c, :], aw[:, c:c + 1], None, ALU.mult)
            ins.then_inc(V.sig(0, "wo"), 1)
            ve.wait_ge(M.sem[0], M.at("bo", 0))
            ve.tensor_copy(w["bo"][:], ps[:, 7, 0:NODES]).then_inc(V.sig(0, "bo"), 1)


LANES = 4
SLOTS = NODES * LANES
TILE = {-1: 0, 0: 1, 1: 2, 2: 3, 3: 4, 4: 0, 5: 2}
RING = 4
PRING = 3
SCALE = DH ** -0.5


def node_chain_phase(nc, a, w, mod_rows, x_mid, out):
    ctx = ExitStack()
    with ctx:
        def sb(name, shape, dt=FP32):
            return ctx.enter_context(nc.sbuf_tensor("b_" + name, shape, dt))

        counts = []

        def count(name, events, slots=SLOTS, by=1):
            counts.append(Count(ctx.enter_context(nc.semaphore("b_" + name)), events, slots, by))
            return counts[-1]

        ident, identb = sb("ident", [P, P]), sb("identb", [P, P], BF16)
        gain, shift = sb("gain", [P, 1, D]), sb("shift", [P, 1, D])
        minus_half, zero, spare = sb("minus_half", [P, CH, 1]), sb("zero", [P, 1]), sb("spare", [P, 1])
        xi = [sb(f"xi{n}", [P, CH, D]) for n in range(2)]
        modi = [sb(f"modi{n}", [P, 2, D]) for n in range(2)]
        xo = [sb(f"xo{n}", [P, CH, D]) for n in range(2)]
        gate = [sb(f"gate{n}", [P, 1, D]) for n in range(2)]
        gated = sb("gated", [P, 2, D])
        node = [[sb(f"node{n}_{i}", [P, T]) for i in range(5)] for n in range(LANES)]
        stats, mv, var, rstd = sb("stats", [P, CH, 6]), sb("mv", [P, CH, 2]), sb("var", [P, CH, 1]), sb("rstd", [P, CH, 1])
        hx = [sb(f"hx{n}", [P, CH, D]) for n in range(2)]
        qf, kf, rest = sb("qf", [P, T]), sb("kf", [P, T]), sb("rest", [P, T])
        qp, kp = ([sb(f"{n}{i}", [P, 3, T], BF16) for i in range(2)] for n in ("qp", "kp"))
        qst, kst = ([sb(f"{n}{i}", [SROWS + 2, MH, T], BF16) for i in range(RING)] for n in ("qst", "kst"))
        vaug = [sb(f"vaug{i}", [P, CH, MH, 2 * DH]) for i in range(RING)]
        mx = [sb(f"mx{i}", [P, MH, CH]) for i in range(2)]
        nm = [sb(f"nm{g}", [P, CH, 2, 4], BF16) for g in range(MG)]
        nrow = [sb(f"nrow{g}", [8, T], BF16) for g in range(MG)]
        prob = [sb(f"prob{i}", [P, 4, T]) for i in range(PRING)]
        ctxu = [sb(f"ctxu{g}", [P, T]) for g in range(MG)]
        rden = sb("rden", [P, CH, 4, 1])
        ctxn, ctxT = sb("ctxn", [P, CH, D]), sb("ctxT", [P, T])
        ps = ctx.enter_context(nc.psum_tensor("b_ps", [P, 8, T], FP32))
        s1_bank = [ps[:, n, :] for n in range(2)]
        s2_bank = [ps[:, 2 + 2 * n:4 + 2 * n, :] for n in range(2)]
        ctx_bank, misc = ps[:, 6, :], ps[:, 7, :]

        loaded = ctx.enter_context(nc.semaphore("b_const_loaded"))
        ones_ready = ctx.enter_context(nc.semaphore("b_ones_ready"))
        filled = ctx.enter_context(nc.semaphore("b_filled"))
        x_in, x_again, stored = ([count(f"{n}{i}", 1, LANES // 2, by) for i in range(2)]
                                 for n, by in (("x_in", 32), ("x_again", 32), ("stored", 16)))
        h_stats, h_aggr, h_eps, h_out = (count(n, 1, LANES) for n in ("h_stats", "h_aggr", "h_eps", "h_out"))
        h_rstd, h_scaled, h_ready, h_turned, n0_ready = (count(n, 1, LANES) for n in
                                                         ("h_rstd", "h_scaled", "h_ready", "h_turned", "n0_ready"))
        o_turned, o_stats, o_aggr, o_eps, o_norm = (count(n, 1, LANES) for n in ("o_turned", "o_stats", "o_aggr", "o_eps", "o_norm"))
        o_rstd, o_gain, o_scaled, o_ready = (count(n, e, LANES) for n, e in (("o_rstd", 1), ("o_gain", 1), ("o_scaled", 2), ("o_ready", 1)))
        k_raw, q_raw, qq_raw, v_raw = (count(n, 1) for n in ("k_raw", "q_raw", "qq_raw", "v_raw"))
        k_ready, q_ready, qq_ready, v_ready = (count(n, 1) for n in ("k_ready", "q_ready", "qq_ready", "v_ready"))
        k_split, q_split = count("k_split", 4), count("q_split", 4)
        k_stacked, q_stacked = ([count(f"{n}{i}", PARTS, SLOTS // 2, 16) for i in range(2)] for n in ("k_stacked", "q_stacked"))
        s1_done, max_done = count("s1_done", MH * CH), count("max_done", MH * CH)
        max_split, max_turned, max_row = count("max_split", 2 * MG), count("max_turned", MG), count("max_row", MG)
        max_stacked = [count(f"max_stacked{g}", 1, by=16) for g in range(MG)]
        UNITS = MG * CH
        s2_done, exp_done, pv_done = count("s2_done", 2 * UNITS), count("exp_done", 2 * UNITS), count("pv_done", UNITS)
        ctx_out, ctx_turned, den_inv, ctx_norm = (count(n, MG) for n in ("ctx_out", "ctx_turned", "den_inv", "ctx_norm"))
        ctx_back, ctxT_ready, o_raw, node_ready = (count(n, 1) for n in ("ctx_back", "ctxT_ready", "o_raw", "node_ready"))
        N_CONST = 16 * 3
        block = ctx.enter_context(nc.Block())

        def lane(s):
            return s % LANES

        def node_of(s):
            return s // LANES % NODES

        def tile(s, n):
            return node[lane(s)][TILE[n]]

        def last_node(s):
            return node_of(s) == NODES - 1

        def wait_node(eng, it, s, n):
            group = s // SLOTS
            if n < 0:
                eng.wait_ge(n0_ready.sem, n0_ready.at(it, group * LANES + lane(s)))
            else:
                eng.wait_ge(node_ready.sem, node_ready.at(it, group * SLOTS + n * LANES + lane(s)))

        INPUT = SLOTS - LANES - 2

        def run(eng, inputs, time):
            for n in range(LANES):
                inputs(0, n)
            for t in range(-3, 1):
                time(0, t, lambda s: s >= 0)
            with eng.Fori(0, B // LANES - 1) as it:
                for t in range(1, SLOTS + 1):
                    time(it, t, lambda s: True)
            for t in range(1, SLOTS + 1):
                time(B // LANES - 1, t, lambda s: s < SLOTS)

        @block.sync
        def _(sync):
            sync.dma_start(ident[:], a["c_ident"]).then_inc(loaded, 16)
            sync.dma_start(gain[:, 0, :], a["ln_g"].rearrange("(a n) -> a n", a=1).broadcast_to([P, D])).then_inc(loaded, 16)
            sync.dma_start(shift[:, 0, :], a["ln_b"].rearrange("(a n) -> a n", a=1).broadcast_to([P, D])).then_inc(loaded, 16)
            for c in counts:
                c.start(sync)

            def stack(it, s, parts, order, split, dst, done):
                sync.wait_ge(split.sem, split.at(it, s, 3))
                for i, part in enumerate(order):
                    src = parts[s % 2][:, part, :]
                    sync.dma_start(dst[s % RING][i * DH:(i + 1) * DH], src).then_inc(done[s % 2].sem, 16)

            def store_max(it, s, g):
                sync.wait_ge(max_row.sem, max_row.at(it, s, g))
                for_h = qst[s % RING][SROWS:SROWS + 2, 4 * g:4 * g + 4, :]
                sync.dma_start(for_h, nrow[g][:]).then_inc(max_stacked[g].sem, 16)

            def load(it, n):
                b = sync.snap(it * LANES + n) if n >= LANES or not isinstance(it, int) else n
                sync.wait_ge(h_turned.sem, h_turned.at(it, n - 2))
                sync.dma_start(xi[n % 2][:], x_mid[bass.ds(b, 1)].rearrange("a (c p) n -> (a p) c n", p=P)).then_inc(x_in[n % 2].sem, 16)
                sync.dma_start(modi[n % 2][:], mod_rows[bass.ds(b, 1), 3 * D:5 * D].rearrange("a (k n) -> a k n", k=2).broadcast_to([P, 2, D])).then_inc(x_in[n % 2].sem, 16)

            def load_again(it, n):
                b = it * LANES + n if isinstance(it, int) else sync.snap(it * LANES + n)
                sync.wait_ge(o_ready.sem, o_ready.at(it, n - 2))
                sync.dma_start(xo[n % 2][:], x_mid[bass.ds(b, 1)].rearrange("a (c p) n -> (a p) c n", p=P)).then_inc(x_again[n % 2].sem, 16)
                sync.dma_start(gate[n % 2][:], mod_rows[bass.ds(b, 1), 5 * D:6 * D].rearrange("a (k n) -> a k n", k=1).broadcast_to([P, 1, D])).then_inc(x_again[n % 2].sem, 16)

            def store(it, n):
                b = it * LANES + n if isinstance(it, int) else sync.snap(it * LANES + n)
                sync.wait_ge(o_ready.sem, o_ready.at(it, n))
                sync.dma_start(out[bass.ds(b, 1)].rearrange("a (c p) n -> (a p) c n", p=P), hx[n % 2][:]).then_inc(stored[n % 2].sem, 16)

            def time(it, t, valid):
                if INPUT <= t < INPUT + LANES and valid(SLOTS):
                    load(it, LANES + t - INPUT)
                if valid(t):
                    store_max(it, t, 1)
                if valid(t + 2):
                    stack(it, t + 2, kp, K_PART, k_split, kst, k_stacked)
                    stack(it, t + 2, qp, Q_PART, q_split, qst, q_stacked)
                if valid(t + 1):
                    store_max(it, t + 1, 0)
                if t >= 1 and last_node(t - 1):
                    load_again(it, lane(t - 1))
                    store(it, lane(t - 1))

            run(sync, load, time)
            for n in range(2):
                sync.wait_ge(stored[n].sem, stored[n].at(B // LANES, -1))

        @block.gpsimd
        def _(gp):
            gp.memset(minus_half[:], -0.5)
            for i in range(RING):
                gp.memset(vaug[i][:], 1.0)
            gp.memset(zero[:], 0.0).then_inc(filled, 1)
            gp.wait_ge(filled, 1)
            gp.wait_ge(loaded, N_CONST)
            gp.tensor_copy(identb[:], ident[:]).then_inc(filled, 1)
            rows = [P, CH, D]

            def input_norm(it, n):
                gp.wait_ge(h_eps.sem, h_eps.at(it, n))
                gp.tensor_tensor(rstd[:], var[:], minus_half[:], ALU.pow).then_inc(h_rstd.sem, 1)
                gp.wait_ge(h_out.sem, h_out.at(it, n))
                gp.tensor_tensor(xi[n % 2][:], xi[n % 2][:], modi[n % 2][:, 1:2, :].broadcast_to(rows), ALU.mult).then_inc(h_scaled.sem, 1)
                gp.wait_ge(h_scaled.sem, h_scaled.at(it, n))
                gp.tensor_tensor(xi[n % 2][:], xi[n % 2][:], modi[n % 2][:, 0:1, :].broadcast_to(rows), ALU.add).then_inc(h_ready.sem, 1)

            def split(it, s, ready, whole, parts, stacked, done, before):
                gp.wait_ge(ready.sem, ready.at(it, s))
                gp.wait_ge(stacked[s % 2].sem, stacked[s % 2].at(it, (s - 2) // 2, PARTS - 1))
                p = parts[s % 2]
                z = zero[:].broadcast_to([P, T])
                gp.tensor_tensor(p[:, 0, :], whole[:], z, ALU.add).then_inc(done.sem, 1)
                gp.wait_ge(done.sem, done.at(it, s, 0))
                gp.wait_ge(before[0].sem, before[0].at(it, before[1], 3))
                gp.tensor_tensor(rest[:], whole[:], p[:, 0, :], ALU.subtract).then_inc(done.sem, 1)
                gp.wait_ge(done.sem, done.at(it, s, 1))
                gp.tensor_tensor(p[:, 1, :], rest[:], z, ALU.add).then_inc(done.sem, 1)
                gp.wait_ge(done.sem, done.at(it, s, 2))
                gp.wait_ge(s2_done.sem, s2_done.at(it, s - RING, 2 * UNITS - 1))
                gp.tensor_tensor(p[:, 2, :], rest[:], p[:, 1, :], ALU.subtract).then_inc(done.sem, 1)

            def output(it, s):
                n = lane(s)
                gp.wait_ge(o_eps.sem, o_eps.at(it, n))
                gp.tensor_tensor(rstd[:], var[:], minus_half[:], ALU.pow).then_inc(o_rstd.sem, 1)
                gp.wait_ge(x_again[n % 2].sem, x_again[n % 2].at(it, n // 2))
                gp.wait_ge(o_scaled.sem, o_scaled.at(it, n - 1, 1))
                gp.tensor_tensor(gated[:, 0:1, :], gate[n % 2][:], gain[:], ALU.mult)
                gp.tensor_tensor(gated[:, 1:2, :], gate[n % 2][:], shift[:], ALU.mult).then_inc(o_gain.sem, 1)
                gp.wait_ge(o_gain.sem, o_gain.at(it, n))
                gp.tensor_tensor(xo[n % 2][:], xo[n % 2][:], gated[:, 1:2, :].broadcast_to(rows), ALU.add).then_inc(o_scaled.sem, 1)
                gp.wait_ge(o_norm.sem, o_norm.at(it, n))
                gp.tensor_tensor(hx[n % 2][:], hx[n % 2][:], gated[:, 0:1, :].broadcast_to(rows), ALU.mult).then_inc(o_scaled.sem, 1)
                gp.wait_ge(o_scaled.sem, o_scaled.at(it, n, 1))
                gp.tensor_tensor(hx[n % 2][:], hx[n % 2][:], xo[n % 2][:], ALU.add).then_inc(o_ready.sem, 1)

            def time(it, t, valid):
                if valid(t + 3):
                    split(it, t + 3, k_ready, kf, kp, k_stacked, k_split, (q_split, t + 2))
                if INPUT <= t < INPUT + LANES and valid(SLOTS):
                    input_norm(it, LANES + t - INPUT)
                if t >= 1 and last_node(t - 1):
                    output(it, t - 1)
                if valid(t + 3):
                    split(it, t + 3, qq_ready, qf, qp, q_stacked, q_split, (k_split, t + 3))

            run(gp, input_norm, time)

        @block.vector
        def _(ve):
            for i in range(RING):
                ins = ve.memset(kst[i][SROWS:SROWS + 2], 1.0)
            ins.then_inc(ones_ready, 1)
            ve.wait_ge(loaded, N_CONST)
            ve.wait_ge(filled, 1)

            def norm(it, n, src, dst, eps, stats_c, aggr_c, eps_c, rstd_c, out_c):
                for c in range(CH):
                    ins = ve.bn_stats(stats[:, c, :], src[:, c, :])
                ins.then_inc(stats_c.sem, 1)
                ve.wait_ge(stats_c.sem, stats_c.at(it, n))
                ve.memset(spare[:], 0.0)
                for c in range(CH):
                    ins = ve.bn_aggr(mv[:, c, :], stats[:, c, :])
                ins.then_inc(aggr_c.sem, 1)
                ve.wait_ge(aggr_c.sem, aggr_c.at(it, n))
                ve.tensor_scalar(var[:], mv[:, :, 1:2], eps, None, ALU.add).then_inc(eps_c.sem, 1)
                ve.wait_ge(rstd_c.sem, rstd_c.at(it, n))
                for c in range(CH):
                    ins = ve.tensor_scalar(dst[:, c, :], src[:, c, :], mv[:, c, 0:1], rstd[:, c, :], ALU.subtract, ALU.mult)
                ins.then_inc(out_c.sem, 1)

            def input_norm(it, n):
                ve.wait_ge(x_in[n % 2].sem, x_in[n % 2].at(it, n // 2))
                norm(it, n, xi[n % 2], xi[n % 2], 1e-5, h_stats, h_aggr, h_eps, h_rstd, h_out)

            def maxima(it, s, half_step):
                for k in (2 * half_step, 2 * half_step + 1):
                    ve.wait_ge(s1_done.sem, s1_done.at(it, s, k))
                    ve.tensor_reduce(mx[s % 2][:, k // CH, k % CH:k % CH + 1], s1_bank[k % 2], AX.X, ALU.max).then_inc(max_done.sem, 1)

            def split_max(it, s, g):
                ve.wait_ge(max_done.sem, max_done.at(it, s, (4 * g + 4) * CH - 1))
                ve.wait_ge(max_turned.sem, max_turned.at(it, s - 1, g))
                m = mx[s % 2][:, 4 * g:4 * g + 4, :].rearrange("p h c -> p c h")
                ve.tensor_scalar(nm[g][:, :, 0, :], m, -1.0, None, ALU.mult).then_inc(max_split.sem, 1)
                ve.wait_ge(max_split.sem, max_split.at(it, s, 2 * g))
                ve.scalar_tensor_tensor(nm[g][:, :, 1, :], m, -1.0, nm[g][:, :, 0, :], ALU.mult, ALU.subtract).then_inc(max_split.sem, 1)

            def normalise(it, s, g):
                ve.wait_ge(ctx_turned.sem, ctx_turned.at(it, s, g))
                turned = misc.rearrange("p (c h w) -> p (c h) w", c=CH, h=4)
                ve.reciprocal(rden[:].rearrange("p c h w -> p (c h) w"), turned[:, :, DH:DH + 1]).then_inc(den_inv.sem, 1)
                ve.wait_ge(den_inv.sem, den_inv.at(it, s, g))
                if g == 0:
                    ve.wait_ge(ctx_back.sem, ctx_back.at(it, s - 1))
                ve.tensor_tensor(ctxn[:, :, 64 * g:64 * g + 64].rearrange("p c (h d) -> p c h d", h=4),
                                 misc.rearrange("p (c h w) -> p c h w", c=CH, h=4)[:, :, :, 0:DH],
                                 rden[:].broadcast_to([P, CH, 4, DH]), ALU.mult).then_inc(ctx_norm.sem, 1)

            def finish_node(it, s):
                ve.wait_ge(o_raw.sem, o_raw.at(it, s))
                c = node_of(s)
                x = tile(s, c)
                ve.scalar_tensor_tensor(x[:], misc, w["bo"][:, c:c + 1], x[:], ALU.add, ALU.add).then_inc(node_ready.sem, 1)

            def values(it, s):
                ve.wait_ge(v_raw.sem, v_raw.at(it, s))
                ve.wait_ge(pv_done.sem, pv_done.at(it, s - RING, UNITS - 1))
                ve.tensor_copy(vaug[s % RING][:, :, :, 0:DH], misc.rearrange("p (c h d) -> p c h d", c=CH, h=MH)).then_inc(v_ready.sem, 1)

            def output(it, s):
                n = lane(s)
                ve.wait_ge(o_turned.sem, o_turned.at(it, n))
                ve.wait_ge(stored[n % 2].sem, stored[n % 2].at(it, n // 2 - 1))
                norm(it, n, misc.rearrange("p (c n) -> p c n", c=CH), hx[n % 2], 1e-6, o_stats, o_aggr, o_eps, o_rstd, o_norm)

            def time(it, t, valid):
                for hs in range(2 * UNITS):
                    if valid(t + 1):
                        maxima(it, t + 1, hs)
                        if hs == 7:
                            split_max(it, t + 1, 0)
                        if hs == 15:
                            split_max(it, t + 1, 1)
                    if hs == 3 and INPUT <= t < INPUT + LANES and valid(SLOTS):
                        input_norm(it, LANES + t - INPUT)
                    if hs == 4 and t >= 1:
                        normalise(it, t - 1, 1)
                    if hs == 8 and t >= 1:
                        finish_node(it, t - 1)
                    if hs == 11 and t >= 1 and last_node(t - 1):
                        output(it, t - 1)
                    if hs == 13 and valid(t):
                        normalise(it, t, 0)
                    if hs == 14 and valid(t + 3):
                        values(it, t + 3)

            run(ve, input_norm, time)

        @block.scalar
        def _(ac):
            ac.wait_ge(loaded, N_CONST)

            def first_node(it, n):
                ac.wait_ge(h_turned.sem, h_turned.at(it, n))
                ac.activation(node[lane(n)][TILE[-1]][:], misc, ACT.Copy).then_inc(n0_ready.sem, 1)

            def exps(it, s, hs):
                n = UNITS * s + hs // 2
                ac.wait_ge(s2_done.sem, s2_done.at(it, s, hs))
                if hs % 2 == 0:
                    m = n - PRING
                    ac.wait_ge(pv_done.sem, pv_done.at(it, m // UNITS, m % UNITS))
                ac.activation(prob[n % PRING][:, 2 * (hs % 2):2 * (hs % 2) + 2, :], s2_bank[hs % 2], ACT.Exp).then_inc(exp_done.sem, 1)

            def keys(it, s):
                c = node_of(s)
                ac.wait_ge(k_raw.sem, k_raw.at(it, s))
                ac.wait_ge(k_split.sem, k_split.at(it, s - 1, 3))
                ac.activation(kf[:], misc, ACT.Identity, bias=w["bk"][:, c:c + 1]).then_inc(k_ready.sem, 1)

            def node_queries(it, s):
                c = node_of(s)
                ac.wait_ge(q_raw.sem, q_raw.at(it, s))
                ac.activation(tile(s, c)[:], misc, ACT.Identity, bias=w["bq"][:, c:c + 1], scale=w["eq"][:, c:c + 1]).then_inc(q_ready.sem, 1)

            def head_queries(it, s):
                ac.wait_ge(qq_raw.sem, qq_raw.at(it, s))
                ac.wait_ge(q_split.sem, q_split.at(it, s - 1, 3))
                ac.activation(qf[:], misc, ACT.Copy, scale=SCALE).then_inc(qq_ready.sem, 1)

            def max_rows(it, s, g):
                ac.wait_ge(max_turned.sem, max_turned.at(it, s, g))
                ac.wait_ge(max_stacked[g].sem, max_stacked[g].at(it, s - 1))
                ac.activation(nrow[g][:], misc.bitcast(BF16)[0:8, 0:T], ACT.Copy).then_inc(max_row.sem, 1)

            def context(it, s, g):
                ac.wait_ge(pv_done.sem, pv_done.at(it, s, CH * g + CH - 1))
                ac.wait_ge(ctx_turned.sem, ctx_turned.at(it, s - 1, g))
                ac.activation(ctxu[g][:], ctx_bank, ACT.Copy).then_inc(ctx_out.sem, 1)

            def context_back(it, s):
                ac.wait_ge(ctx_back.sem, ctx_back.at(it, s))
                ac.wait_ge(o_raw.sem, o_raw.at(it, s - 1))
                ac.activation(ctxT[:], misc, ACT.Copy).then_inc(ctxT_ready.sem, 1)

            def time(it, t, valid):
                for hs in range(2 * UNITS):
                    if valid(t):
                        exps(it, t, hs)
                    if hs == 1 and t >= 1:
                        context(it, t - 1, 1)
                    if hs == 1 and valid(t + 3):
                        keys(it, t + 3)
                    if hs == 2 and valid(t):
                        max_rows(it, t, 1)
                    if hs == 5 and INPUT + 1 <= t < INPUT + 1 + LANES and valid(SLOTS):
                        first_node(it, LANES + t - INPUT - 1)
                    if hs == 6 and t >= 1:
                        context_back(it, t - 1)
                    if hs == 9 and valid(t):
                        context(it, t, 0)
                    if hs == 9 and valid(t + 1):
                        max_rows(it, t + 1, 0)
                    if hs == 10 and valid(t + 3):
                        node_queries(it, t + 3)
                    if hs == 12 and valid(t + 3):
                        head_queries(it, t + 3)

            run(ac, first_node, time)

        @block.tensor
        def _(pe):
            pe.wait_ge(loaded, N_CONST)
            pe.wait_ge(filled, 2)
            pe.wait_ge(ones_ready, 1)
            free = [None]

            def shared(it, reader, s, k=0):
                if free[0]:
                    c, s0, k0 = free[0]
                    pe.wait_ge(c.sem, c.at(it, s0, k0))
                free[0] = (reader, s, k)

            def transposes(src):
                for c in range(CH):
                    ins = pe.transpose(misc[:, c * P:(c + 1) * P], src[:, c * P:(c + 1) * P], ident[:])
                return ins

            def first_node(it, n):
                shared(it, n0_ready, n)
                pe.wait_ge(h_ready.sem, h_ready.at(it, n))
                transposes(xi[n % 2][:].rearrange("p c n -> p (c n)")).then_inc(h_turned.sem, 1)

            def scores_by_query(it, s, hs):
                h = hs // 2
                for k in (2 * hs, 2 * hs + 1):
                    if k == 0:
                        pe.wait_ge(k_stacked[s % 2].sem, k_stacked[s % 2].at(it, s // 2, PARTS - 1))
                        pe.wait_ge(q_stacked[s % 2].sem, q_stacked[s % 2].at(it, s // 2, PARTS - 1))
                    m = s * MH * CH + k - 2
                    pe.wait_ge(max_done.sem, max_done.at(it, m // (MH * CH), m % (MH * CH)))
                    c = k % CH
                    pe.matmul(s1_bank[k % 2], qst[s % RING][0:SROWS, h, c * P:(c + 1) * P], kst[s % RING][0:SROWS, h, :],
                              start=True, stop=True).then_inc(s1_done.sem, 1)

            def scores_by_key(it, s, hs):
                u = hs // 2
                g, c = u // CH, u % CH
                if hs % (2 * CH) == 0:
                    pe.wait_ge(max_stacked[g].sem, max_stacked[g].at(it, s))
                m = s * 2 * UNITS + hs - 2
                pe.wait_ge(exp_done.sem, exp_done.at(it, m // (2 * UNITS), m % (2 * UNITS)))
                for j in range(2):
                    h = 4 * g + 2 * (hs % 2) + j
                    ins = pe.matmul(s2_bank[hs % 2][:, j, :], kst[s % RING][:, h, c * P:(c + 1) * P], qst[s % RING][:, h, :],
                                    start=True, stop=True)
                ins.then_inc(s2_done.sem, 1)

            def weigh_values(it, s, u):
                g, c = u // CH, u % CH
                pe.wait_ge(exp_done.sem, exp_done.at(it, s, 2 * u + 1))
                if c == 0:
                    if g:
                        pe.wait_ge(ctx_out.sem, ctx_out.at(it, s, 0))
                    else:
                        pe.wait_ge(ctx_out.sem, ctx_out.at(it, s - 1, 1))
                        pe.wait_ge(v_ready.sem, v_ready.at(it, s))
                for j in range(4):
                    ins = pe.matmul(ctx_bank[32 * j:32 * j + 32, :], vaug[s % RING][:, c, 4 * g + j, :], prob[(UNITS * s + u) % PRING][:, j, :],
                                    start=(c == 0), stop=(c == CH - 1))
                ins.then_inc(pv_done.sem, 1)

            def turn_max(it, s, g):
                shared(it, max_row, s, g)
                pe.wait_ge(max_split.sem, max_split.at(it, s, 2 * g + 1))
                for c in range(CH):
                    ins = pe.transpose(misc.bitcast(BF16)[0:8, c * P:(c + 1) * P], nm[g][:, c].rearrange("p a h -> p (a h)"), identb[:])
                ins.then_inc(max_turned.sem, 1)

            def turn_context(it, s, g):
                shared(it, ctx_norm, s, g)
                pe.wait_ge(ctx_out.sem, ctx_out.at(it, s, g))
                transposes(ctxu[g]).then_inc(ctx_turned.sem, 1)

            def turn_back(it, s):
                shared(it, ctxT_ready, s)
                pe.wait_ge(ctx_norm.sem, ctx_norm.at(it, s, 1))
                transposes(ctxn[:].rearrange("p c n -> p (c n)")).then_inc(ctx_back.sem, 1)

            def project_out(it, s):
                shared(it, node_ready, s)
                pe.wait_ge(ctxT_ready.sem, ctxT_ready.at(it, s))
                pe.matmul(misc, w["wo"][:, node_of(s), :], ctxT[:], start=True, stop=True).then_inc(o_raw.sem, 1)

            def keys(it, s):
                c = node_of(s)
                n = WIRING[c][1][1]
                shared(it, k_ready, s)
                wait_node(pe, it, s, n)
                pe.matmul(misc, w["wk"][:, c, :], tile(s, n)[:], start=True, stop=True).then_inc(k_raw.sem, 1)

            def node_queries(it, s):
                c = node_of(s)
                n = WIRING[c][1][0]
                shared(it, q_ready, s)
                wait_node(pe, it, s, n)
                pe.matmul(misc, w["wqe"][:, c, :], tile(s, n)[:], start=True, stop=True).then_inc(q_raw.sem, 1)

            def head_queries(it, s):
                c = node_of(s)
                shared(it, qq_ready, s)
                pe.wait_ge(q_ready.sem, q_ready.at(it, s))
                pe.matmul(misc, w["wq"][:, c, :], tile(s, c)[:], start=True, stop=True).then_inc(qq_raw.sem, 1)

            def values(it, s):
                c = node_of(s)
                n = WIRING[c][1][2]
                shared(it, v_ready, s)
                wait_node(pe, it, s, n)
                for k in range(CH):
                    ins = pe.matmul(misc[:, k * D:(k + 1) * D], tile(s, n)[:, k * P:(k + 1) * P], w["wv"][:, c, :], start=True, stop=True)
                ins.then_inc(v_raw.sem, 1)

            def output(it, s):
                shared(it, o_norm, lane(s))
                pe.wait_ge(node_ready.sem, node_ready.at(it, s))
                transposes(tile(s, NODES - 1)).then_inc(o_turned.sem, 1)

            def time(it, t, valid):
                if t == 1:
                    free[0] = (v_ready, LANES - 1, 0)
                for hs in range(2 * UNITS):
                    if valid(t):
                        scores_by_key(it, t, hs)
                    if valid(t + 1):
                        scores_by_query(it, t + 1, hs)
                    if hs % 2 == 1:
                        if hs > 1 and valid(t):
                            weigh_values(it, t, hs // 2 - 1)
                        if hs == 1 and t >= 1:
                            weigh_values(it, t - 1, UNITS - 1)
                    if hs == 1 and valid(t + 3):
                        keys(it, t + 3)
                    if hs == 2 and valid(t):
                        turn_max(it, t, 1)
                    if hs == 4 and t >= 1:
                        turn_context(it, t - 1, 1)
                    if hs == 5 and INPUT + 1 <= t < INPUT + 1 + LANES and valid(SLOTS):
                        first_node(it, LANES + t - INPUT - 1)
                    if hs == 6 and t >= 1:
                        turn_back(it, t - 1)
                    if hs == 8 and t >= 1:
                        project_out(it, t - 1)
                    if hs == 9 and valid(t + 1):
                        turn_max(it, t + 1, 0)
                    if hs == 10 and valid(t + 3):
                        node_queries(it, t + 3)
                    if hs == 11 and t >= 1 and last_node(t - 1):
                        output(it, t - 1)
                    if hs == 12 and valid(t + 3):
                        head_queries(it, t + 3)
                    if hs == 13 and valid(t):
                        turn_context(it, t, 0)
                    if hs == 14 and valid(t + 3):
                        values(it, t + 3)

            run(pe, first_node, time)


def build(nc, a, out):
    mod_rows = nc.dram_tensor("mod_rows", (B, 6 * D), FP32, kind="Internal").ap()
    x_mid = nc.dram_tensor("x_mid", (B, T, D), FP32, kind="Internal").ap()
    modulation_phase(nc, a, mod_rows)
    decay_attention_phase(nc, a, mod_rows, x_mid)
    ctx = ExitStack()
    with ctx:
        w = {n: ctx.enter_context(nc.sbuf_tensor("chain_" + n, [P, NODES, D], FP32)) for n in ("wqe", "wq", "wk", "wv", "wo")}
        w |= {n: ctx.enter_context(nc.sbuf_tensor("chain_" + n, [P, NODES], FP32)) for n in ("bq", "bk", "bo", "eq")}
        chain_weights(nc, a, w)
        node_chain_phase(nc, a, w, mod_rows, x_mid, out)


_ATTN = ["x", "q_w", "q_b", "k_w", "k_b", "v_w", "v_b", "o_w", "o_b", "ln1_w", "ln1_b", "ln2_w", "ln2_b",
         "dec_w", "dec_b", "f1_w", "f1_b", "f2_w", "f2_b"]
_CHAIN = ["ew", "act_w", "We", "be", "Wq", "Wk", "Wv", "Wo", "ln_g", "ln_b"]


def constants():
    p = np.arange(P)
    c = {"c_ident": np.eye(P), "c_upto": p[:, None] <= p[None, :], "c_after": p[:, None] > p[None, :],
         "c_headmask": p[:, None] // LK == np.arange(LH)}
    c["c_blockmask"] = np.repeat(c["c_headmask"][:, :, None], LW, 2)
    c["c_pick"] = np.arange(96)[:, None] % 32 == np.arange(LH)
    same = p[:, None] // 32 == p[None, :] // 32
    c["c_denrow_a"] = same & (p[:, None] % 32 == LK)
    c["c_denrow_b"] = same & (p[:, None] % 32 == DH)
    c["c_floor"] = np.where(p % 32 // LK == 1, LION_EPS, np.finfo(np.float32).min)[:, None]
    c = {k: np.ascontiguousarray(v, dtype=np.float32) for k, v in c.items()}
    return c


def kernel(**inputs):
    import concourse.bacc as bacc
    from concourse.bass_utils import run_bass_kernel_spmd

    nc = bacc.Bacc("TRN2", target_bir_lowering=False, num_devices=1)
    given = {n: inputs["L0_attn_" + n] for n in _ATTN}
    given |= {n: inputs["L0_ffn_" + n] for n in _CHAIN}
    given |= {"c": inputs["L0_c"], "wmod": inputs["L0_wmod"]}
    given |= constants()
    arrays, aps = {}, {}
    for name, value in given.items():
        arrays[f"in_{name}"] = v = np.ascontiguousarray(value)
        aps[name] = nc.dram_tensor(f"in_{name}", v.shape, mybir.dt.from_np(v.dtype), kind="ExternalInput").ap()
    out = nc.dram_tensor("out", (B, T, D), FP32, kind="ExternalOutput").ap()
    build(nc, aps, out)
    r = run_bass_kernel_spmd(nc, [arrays], core_ids=[0])
    return r.results[0]["out"]
```

```python
import numpy as np
import concourse.bass as bass
from concourse import mybir
from contextlib import ExitStack

FP32 = mybir.dt.float32
BF16 = mybir.dt.bfloat16
ALU = mybir.AluOpType
ACT = mybir.ActivationFunctionType
AX = mybir.AxisListType

P = 128
B, T, D = 16, 512, 128
CH = T // P

LH, LK = 16, 8
FFN = 512
FC = FFN // P
LION_EPS, LAM_MIN = 1e-6, 1e-8
LW = 2 * LK
LR = LH // 4
HEADS_FROM, HEAD_TIME = 33.7, 3.56
DONE = HEADS_FROM + HEAD_TIME * LH
TIMES = DONE + 33.1

NODES, MAX_PREV = 6, 5
MH, DH = 8, 16
MG = MH // 4
PARTS = 6
SROWS = PARTS * DH
K_PART = (0, 0, 1, 1, 0, 2)
Q_PART = (0, 1, 0, 1, 2, 0)


def node_inputs():
    out, first = [], 0
    for c in range(NODES):
        n = min(c + 1, MAX_PREV)
        out.append(((first + n - 1, first, first + n // 2), (c - 1, c - n, c - n + n // 2)))
        first += n
    return out


WIRING = node_inputs()


class Steps:

    def __init__(self, sem, names):
        self.sem, self.names = sem, names
        self.place = {n: i for i, n in enumerate(names)}
        assert len(self.place) == len(names)
        self.next = [0] * len(sem)

    def sig(self, lane, name):
        assert self.names[self.next[lane]] == name, (self.names[self.next[lane]], name)
        self.next[lane] = (self.next[lane] + 1) % len(self.names)
        return self.sem[lane]

    def at(self, name, it):
        return it * len(self.names) + self.place[name] + 2

    def all(self, it):
        return it * len(self.names) + 1

    def start(self, eng):
        for sem in self.sem:
            eng.sem_inc(sem, 1)


def modulation_phase(nc, a, mod_rows):
    ctx = ExitStack()
    with ctx:
        def sb(name, shape, dt=FP32):
            return ctx.enter_context(nc.sbuf_tensor("m_" + name, shape, dt))

        def sem(name):
            return ctx.enter_context(nc.semaphore("m_" + name))

        cT, wmod = sb("cT", [D, B]), sb("wmod", [D, 6 * D])
        ex, one_ex, silu = sb("ex", [D, B]), sb("one_ex", [D, B]), sb("silu", [D, B])
        mod = sb("mod", [B, 6, D])
        sign, size = sb("sign", [B, 2, D]), sb("size", [B, 2, D])
        ps = ctx.enter_context(nc.psum_tensor("m_ps", [P, 2, 512], FP32))
        loaded, exp_done, dve_done, mod_summed, stored = (sem(n) for n in ("loaded", "exp_done", "dve_done", "mod_summed", "stored"))
        gates = mod[:, 2::3, :]
        block = ctx.enter_context(nc.Block())

        @block.sync
        def _(sync):
            sync.dma_start(cT[:], a["c"].rearrange("b d -> d b"), allow_slow_non_contiguous=True).then_inc(loaded, 16)
            sync.dma_start(wmod[:], a["wmod"]).then_inc(loaded, 16)
            sync.wait_ge(dve_done, 11)
            sync.dma_start(mod_rows, mod[:].rearrange("b k n -> b (k n)")).then_inc(stored, 16)
            sync.wait_ge(stored, 16)

        @block.scalar
        def _(ac):
            ac.wait_ge(loaded, 32)
            ac.activation(ex[:], cT[:], ACT.Exp, scale=-1.0).then_inc(exp_done, 1)

        @block.tensor
        def _(pe):
            pe.wait_ge(dve_done, 3)
            for k in range(2):
                ins = pe.matmul(ps[0:B, k, 0:3 * D], silu[:], wmod[:, k * 3 * D:(k + 1) * 3 * D], start=True, stop=True)
            ins.then_inc(mod_summed, 1)

        @block.vector
        def _(ve):
            ve.wait_ge(exp_done, 1)
            ve.tensor_scalar(one_ex[:], ex[:], 1.0, None, ALU.add).then_inc(dve_done, 1)
            ve.wait_ge(dve_done, 1)
            ve.reciprocal(ex[:], one_ex[:]).then_inc(dve_done, 1)
            ve.wait_ge(dve_done, 2)
            ve.tensor_tensor(silu[:], cT[:], ex[:], ALU.mult).then_inc(dve_done, 1)
            ve.wait_ge(mod_summed, 1)
            for k in range(2):
                ve.tensor_copy(mod[:, 3 * k:3 * k + 3, :].rearrange("b k n -> b (k n)"), ps[0:B, k, 0:3 * D]).then_inc(dve_done, 1)
            ve.wait_ge(dve_done, 5)
            for k in (1, 4):
                ve.tensor_scalar(mod[:, k, :], mod[:, k, :], 1.0, None, ALU.add).then_inc(dve_done, 1)
            ve.tensor_scalar(sign[:], gates, 0.0, 2.0, ALU.is_ge, ALU.mult).then_inc(dve_done, 1)
            ve.scalar_tensor_tensor(size[:], gates, -1.0, gates, ALU.mult, ALU.max).then_inc(dve_done, 1)
            ve.wait_ge(dve_done, 9)
            ve.tensor_scalar(size[:], size[:], 0.25, None, ALU.max).then_inc(dve_done, 1)
            ve.wait_ge(dve_done, 10)
            ve.scalar_tensor_tensor(gates, sign[:], -1.0, size[:], ALU.add, ALU.mult).then_inc(dve_done, 1)


def decay_attention_phase(nc, a, mod_rows, x_mid):
    ctx = ExitStack()
    with ctx:
        def sb(name, shape, dt=FP32):
            return ctx.enter_context(nc.sbuf_tensor("a_" + name, shape, dt))

        def sems(name):
            return [ctx.enter_context(nc.semaphore(f"a_{name}{p}")) for p in range(2)]

        ident = sb("ident", [P, P])
        upto = sb("upto", [P, P])
        after = sb("after", [P, P])
        blockmask = sb("blockmask", [P, LH, LW])
        headmask = sb("headmask", [P, LH])
        pick = sb("pick", [96, LH, P], BF16)
        unpick = sb("unpick", [96, LH, P], BF16)
        spare = sb("spare", [P, 1])
        pick1 = sb("pick1", [96, LH])
        cols = sb("cols", [P, 6])
        rows = sb("rows", [P, 3, D])
        decb = sb("decb", [P, LH])
        f1b = sb("f1b", [P, FC])
        qw, kw, vw = sb("qw", [P, D]), sb("kw", [P, D]), sb("vw", [P, D])
        decw = sb("decw", [P, LH])
        ow = sb("ow", [P, D])
        f1w = sb("f1w", [P, FFN])
        f2w = sb("f2w", [P, FC, D])

        def two(name, shape, dt=FP32):
            return [sb(f"{name}{p}", shape, dt) for p in range(2)]

        x = two("x", [P, CH, D])
        modb = two("modb", [P, 3, D])
        stats, mv = two("stats", [P, CH, 6]), two("mv", [P, CH, 2])
        var, rstd = two("var", [P, CH, 1]), two("rstd", [P, CH, 1])
        minus_half = sb("minus_half", [P, CH, 1])
        xn, h, hn, hob = (two(n, [P, CH, D]) for n in ("xn", "h", "hn", "hob"))
        xnT = two("xnT", [P, T])
        hidden = two("hidden", [P, FC, T])
        tq, rq, tk, rk = ([hidden[p][:, i, :] for p in range(2)] for i in range(4))
        phiq, phik = two("phiq", [P, T]), two("phik", [P, T])
        zb, ez, lnz, ll = (two(n, [P, CH, LH]) for n in ("zb", "ez", "lnz", "ll"))
        ll3 = two("ll3", [P, CH, 3, 32])
        llrep = two("llrep", [P, CH, LH, LK])
        vaug = two("vaug", [P, CH, LH + 1, LW])
        cum3 = two("cum3", [96, T], BF16)
        cumr = two("cumr", [96, T])
        e1t, e2t = two("e1t", [P, T]), two("e2t", [P, T])
        etok = two("etok", [P, 2, CH, LH])
        kf, kb = two("kf", [P, CH, LH, LK]), two("kb", [P, CH, LH, LK])
        st = two("st", [P, 6, LH, LW])
        stp = two("stp", [P, 6, LR, 4, 32])
        qf, qb = two("qf", [P, T]), two("qb", [P, T])
        qm = two("qm", [P, 2, T])
        absd, dec, at = two("absd", [P, 2, T]), two("dec", [P, 2, T]), two("at", [P, 2, T])
        un = two("un", [P, T])
        rden = two("rden", [P, CH, 4, 1])
        attn, attnT = two("attn", [P, CH, LR, 4, LK]), two("attnT", [P, T])
        ps = ctx.enter_context(nc.psum_tensor("a_ps", [P, 8, T], FP32))

        def bank(p, n):
            return ps[:, 4 * p + n, :]

        def chunked(ap):
            return ap.rearrange("p (c n) -> p c n", c=CH)

        ld_const = ctx.enter_context(nc.semaphore("a_const_loaded"))
        picks_ready = ctx.enter_context(nc.semaphore("a_picks_ready"))
        pads_zero = ctx.enter_context(nc.semaphore("a_pads_zero"))
        x_loaded, x_stored = sems("x_loaded"), sems("x_stored")
        heads, rounds = range(LH), range(LR)

        def norm(tag):
            return [tag + s for s in ("stats", "aggr", "eps", "out")]

        def divided(r):
            return [f"floor{r}", f"inv{r}", f"attn{r}"]

        V = Steps(sems("vector_steps"), norm("ln1") + norm("ln2") + ["tq", "tk", "zb", "vaug", "ll", "ll3", "llrep",
                  "ct1", "ct2", "ct3", "ct4", "kf", "kb", "s1", "r2", "s2", "s3", "r1", "r0"]
                  + ["mask0"] + sum([([f"mask{i + 1}"] if i + 1 < LH else []) + [f"at{i}"] + (divided((i - 6) // 4) if i >= 6 and i % 4 == 2 else []) for i in heads], [])
                  + divided(LR - 1) + ["x1"] + norm("ln3") + ["y"])
        S = Steps(sems("scalar_steps"), ["xnT", "rq", "rk", "eq", "ek", "ez", "lnz", "e1t", "e2t", "etok"]
                  + sum([([f"un{(i - 5) // 4}"] if i >= 5 and i % 4 == 1 else []) + [f"abs{i}", f"dec{i}"] for i in heads], [])
                  + [f"un{LR - 1}", "attnT", "xn2T"] + [f"gelu{m}" for m in range(FC)])
        G = Steps(sems("gpsimd_steps"), ["ln1rstd", "h1", "h", "ln2rstd", "hob", "phiq", "phik", "qf", "qb"]
                  + [f"sp{i}" for i in range(6)]
                  + ["ln3rstd", "x1f", "gy", "xo"])
        M = Steps(sems("tensor_steps"), ["tr1", "qT", "kT", "dec", "v", "ct", "ce1", "ce2", "tok", "ktok",
                  "F01", "F2G3", "G12", "diff0", "scores0", "inter0"]
                  + sum([[f"diff{i}", f"scores{i}", f"intra{i - 1}"] + ([f"inter{i // 4}"] if i % 4 == 0 else [])
                         + ([f"turn{(i - 6) // 4}"] if i >= 6 and i % 4 == 2 else []) for i in heads[1:]], [])
                  + [f"intra{LH - 1}", f"turn{LR - 1}", "back", "oproj", "tr2"] + [f"f1_{m}" for m in range(FC)] + ["f2"])
        N_CONST = 16 * (14 + 6 + 3 + 1)
        block = ctx.enter_context(nc.Block())

        def head_time(i):
            return HEADS_FROM + HEAD_TIME * i

        def run(eng, stages):
            half = round(TIMES / 2, 2)
            times = np.maximum.accumulate([t for t, _ in stages])
            stages = [(round(float(t), 2), s) for t, (_, s) in zip(times, stages)]
            early = [(t, s) for t, s in stages if t < half]
            late = [(round(t - half, 2), s) for t, s in stages if t >= half]

            def merged(it0, stages0, it1, stages1):
                steps = [(t, 0, i, it0, s) for i, (t, s) in enumerate(stages0)] + [(t, 1, i, it1, s) for i, (t, s) in enumerate(stages1)]
                for _, p, _, it, stage in sorted(steps, key=lambda step: step[:3]):
                    stage(it, p)

            last = B // 2 - 1
            merged(0, early, 0, [])
            with eng.Fori(0, last) as it:
                merged(it, late, it, early)
                merged(it + 1, early, it, late)
            merged(last, late, last, early)
            merged(last, [], last, late)

        @block.sync
        def _(sync):
            loads = [
                (ident, a["c_ident"]), (upto, a["c_upto"]), (after, a["c_after"]),
                (blockmask, a["c_blockmask"]), (headmask, a["c_headmask"]), (pick1, a["c_pick"]),
                (qw, a["q_w"]), (kw, a["k_w"]), (vw, a["v_w"]), (decw, a["dec_w"]), (ow, a["o_w"]), (f1w, a["f1_w"]),
                (f2w, a["f2_w"].rearrange("(m p) n -> p m n", p=P)),
                (f1b, a["f1_b"].rearrange("(m p) -> p m", p=P)),
            ]
            for dst, src in loads:
                sync.dma_start(dst[:], src, allow_slow_non_contiguous=True).then_inc(ld_const, 16)
            for i, n in enumerate(("ln1_w", "ln1_b", "ln2_w", "ln2_b", "q_b", "k_b")):
                sync.dma_start(cols[:, i:i + 1], a[n].rearrange("(p a) -> p a", a=1)).then_inc(ld_const, 16)
            for i, n in enumerate(("v_b", "o_b", "f2_b")):
                sync.dma_start(rows[:, i, :], a[n].rearrange("(a n) -> a n", a=1).broadcast_to([P, D])).then_inc(ld_const, 16)
            sync.dma_start(decb[:], a["dec_b"].rearrange("(a n) -> a n", a=1).broadcast_to([P, LH])).then_inc(ld_const, 16)
            for steps in (M, V, S, G):
                steps.start(sync)
            for p in range(2):
                sync.sem_inc(x_stored[p], 16)

            def s_load(it, p):
                b = it * 2 + p
                sync.wait_ge(G.sem[p], G.all(it))
                sync.dma_start(x[p][:], a["x"][bass.ds(b, 1)].rearrange("a (c p) n -> (a p) c n", p=P)).then_inc(x_loaded[p], 16)
                sync.dma_start(modb[p][:], mod_rows[bass.ds(b, 1), 0:3 * D].rearrange("a (k n) -> a k n", k=3).broadcast_to([P, 3, D])).then_inc(x_loaded[p], 16)

            def s_store(it, p):
                b = it * 2 + p
                sync.wait_ge(G.sem[p], G.at("xo", it))
                sync.dma_start(x_mid[bass.ds(b, 1)].rearrange("a (c p) n -> (a p) c n", p=P), xn[p][:]).then_inc(x_stored[p], 16)

            run(sync, [(4.3, s_load), (DONE + 7.7, s_store)])
            for p in range(2):
                sync.wait_ge(x_stored[p], 16 * (B // 2) + 16)

        @block.gpsimd
        def _(gp):
            def inverse_root(it, p, tag):
                gp.wait_ge(V.sem[p], V.at(tag + "eps", it))
                gp.tensor_tensor(rstd[p][:], var[p][:], minus_half[:], ALU.pow).then_inc(G.sig(p, tag + "rstd"), 1)

            def s_rstd1(it, p):
                inverse_root(it, p, "ln1")

            def s_h(it, p):
                gp.wait_ge(x_loaded[p], it * 32 + 32)
                gp.wait_ge(V.sem[p], V.at("ln1out", it))
                gp.tensor_tensor(xn[p][:], xn[p][:], modb[p][:, 1:2, :].broadcast_to([P, CH, D]), ALU.mult).then_inc(G.sig(p, "h1"), 1)
                gp.wait_ge(G.sem[p], G.at("h1", it))
                gp.tensor_tensor(h[p][:], xn[p][:], modb[p][:, 0:1, :].broadcast_to([P, CH, D]), ALU.add).then_inc(G.sig(p, "h"), 1)

            def s_hob(it, p):
                inverse_root(it, p, "ln2")
                gp.tensor_tensor(hob[p][:], h[p][:], rows[:, 1:2, :].broadcast_to([P, CH, D]), ALU.add).then_inc(G.sig(p, "hob"), 1)

            def s_phi(it, p):
                gp.wait_ge(S.sem[p], S.at("eq", it))
                gp.tensor_tensor(phiq[p][:], rq[p], tq[p], ALU.add).then_inc(G.sig(p, "phiq"), 1)
                gp.wait_ge(S.sem[p], S.at("ek", it))
                gp.tensor_tensor(phik[p][:], rk[p], tk[p], ALU.add).then_inc(G.sig(p, "phik"), 1)

            def s_q(it, p):
                gp.wait_ge(G.sem[p], G.at("phiq", it))
                gp.wait_ge(S.sem[p], S.at("e2t", it))
                gp.tensor_tensor(qf[p][:], phiq[p][:], e1t[p][:], ALU.mult).then_inc(G.sig(p, "qf"), 1)
                gp.tensor_tensor(qb[p][:], phiq[p][:], e2t[p][:], ALU.mult).then_inc(G.sig(p, "qb"), 1)

            def s_states(it, p):
                for i, name in enumerate(("s1", "s2", "s3", "r0", "r1", "r2")):
                    gp.wait_ge(V.sem[p], V.at(name, it))
                    gp.tensor_tensor(stp[p][:, i].rearrange("p r g w -> p (r g) w")[:, :, 0:LW], st[p][:, i], blockmask[:], ALU.mult).then_inc(G.sig(p, f"sp{i}"), 1)

            def s_x1f(it, p):
                inverse_root(it, p, "ln3")
                gp.tensor_tensor(hob[p][:], h[p][:], rows[:, 2:3, :].broadcast_to([P, CH, D]), ALU.add).then_inc(G.sig(p, "x1f"), 1)

            def s_out(it, p):
                gp.wait_ge(V.sem[p], V.at("y", it))
                gp.tensor_tensor(hn[p][:], hn[p][:], modb[p][:, 2:3, :].broadcast_to([P, CH, D]), ALU.mult).then_inc(G.sig(p, "gy"), 1)
                gp.wait_ge(G.sem[p], G.at("gy", it))
                gp.tensor_tensor(xn[p][:], hn[p][:], x[p][:], ALU.add).then_inc(G.sig(p, "xo"), 1)

            for p in range(2):
                gp.memset(ll3[p][:], 0.0)
                gp.memset(stp[p][:], 0.0)
                gp.memset(vaug[p][:, :, 0:LH, :], 1.0)
                gp.memset(vaug[p][:, :, LH:LH + 1, :], 0.0)
            gp.memset(minus_half[:], -0.5).then_inc(pads_zero, 1)
            gp.wait_ge(ld_const, N_CONST)
            run(gp, [(7.5, s_rstd1), (7.5, s_h), (7.5, s_hob), (19.3, s_phi), (19.3, s_q), (19.3, s_states)]
                + [(DONE + 8.3, s_x1f), (DONE + 45.0, s_out)])

        @block.vector
        def _(ve):
            def norm_steps(it, p, tag, src, dst, eps):
                for c in range(CH):
                    ins = ve.bn_stats(stats[p][:, c, :], src[:, c, :])
                ins.then_inc(V.sig(p, tag + "stats"), 1)
                ve.wait_ge(V.sem[p], V.at(tag + "stats", it))
                ve.memset(spare[:], 0.0)
                for c in range(CH):
                    ins = ve.bn_aggr(mv[p][:, c, :], stats[p][:, c, :])
                ins.then_inc(V.sig(p, tag + "aggr"), 1)
                ve.wait_ge(V.sem[p], V.at(tag + "aggr", it))
                ve.tensor_scalar(var[p][:], mv[p][:, :, 1:2], eps, None, ALU.add).then_inc(V.sig(p, tag + "eps"), 1)
                ve.wait_ge(G.sem[p], G.at(tag + "rstd", it))
                for c in range(CH):
                    ins = ve.tensor_scalar(dst[:, c, :], src[:, c, :], mv[p][:, c, 0:1], rstd[p][:, c, :], ALU.subtract, ALU.mult)
                ins.then_inc(V.sig(p, tag + "out"), 1)

            def s_ln1(it, p):
                ve.wait_ge(x_loaded[p], it * 32 + 32)
                ve.wait_ge(x_stored[p], it * 16 + 16)
                norm_steps(it, p, "ln1", x[p], xn[p], 1e-5)

            def s_ln2(it, p):
                ve.wait_ge(G.sem[p], G.at("h", it))
                norm_steps(it, p, "ln2", h[p], hn[p], 1e-5)

            def s_tq(it, p):
                ve.wait_ge(M.sem[p], M.at("qT", it))
                ve.tensor_scalar(tq[p], bank(p, 1), cols[:, 4:5], 0.0, ALU.add, ALU.min).then_inc(V.sig(p, "tq"), 1)

            def s_tk(it, p):
                ve.wait_ge(M.sem[p], M.at("kT", it))
                ve.tensor_scalar(tk[p], bank(p, 2), cols[:, 5:6], 0.0, ALU.add, ALU.min).then_inc(V.sig(p, "tk"), 1)

            def s_zb(it, p):
                ve.wait_ge(M.sem[p], M.at("dec", it))
                ve.tensor_tensor(zb[p][:], bank(p, 3)[:, 0:CH * LH].rearrange("p (c h) -> p c h", c=CH),
                                 decb[:].rearrange("p (a h) -> p a h", a=1).broadcast_to([P, CH, LH]), ALU.add).then_inc(V.sig(p, "zb"), 1)

            def s_vaug(it, p):
                ve.wait_ge(M.sem[p], M.at("v", it))
                ve.tensor_tensor(vaug[p][:, :, 0:LH, 0:LK], bank(p, 0).rearrange("p (c h v) -> p c h v", c=CH, h=LH),
                                 rows[:, 0:1, :].rearrange("p a (h v) -> p a h v", h=LH).broadcast_to([P, CH, LH, LK]), ALU.add).then_inc(V.sig(p, "vaug"), 1)

            def s_ll(it, p):
                ve.wait_ge(S.sem[p], S.at("lnz", it))
                ve.tensor_scalar(ll[p][:], lnz[p][:], -1.0, float(np.log(LAM_MIN)), ALU.mult, ALU.max).then_inc(V.sig(p, "ll"), 1)
                ve.wait_ge(V.sem[p], V.at("ll", it))
                ve.tensor_copy(ll3[p][:, :, :, 0:LH], ll[p][:].rearrange("p c (a h) -> p c a h", a=1).broadcast_to([P, CH, 3, LH])).then_inc(V.sig(p, "ll3"), 1)
                ve.tensor_copy(llrep[p][:], ll[p][:].rearrange("p c (h a) -> p c h a", a=1).broadcast_to([P, CH, LH, LK])).then_inc(V.sig(p, "llrep"), 1)

            def s_cum(it, p):
                ve.wait_ge(M.sem[p], M.at("ct", it))
                ve.tensor_copy(cum3[p][:], bank(p, 3)[0:96, :]).then_inc(V.sig(p, "ct1"), 1)
                ve.wait_ge(V.sem[p], V.at("ct1", it))
                ve.tensor_tensor(cumr[p][:], bank(p, 3)[0:96, :], cum3[p][:], ALU.subtract).then_inc(V.sig(p, "ct2"), 1)
                ve.wait_ge(V.sem[p], V.at("ct2", it))
                ve.tensor_copy(cum3[p][32:64, :], cumr[p][32:64, :])
                ve.tensor_copy(cum3[p][64:96, :], cumr[p][64:96, :]).then_inc(V.sig(p, "ct3"), 1)
                ve.wait_ge(V.sem[p], V.at("ct3", it))
                ve.tensor_tensor(cum3[p][64:96, :], cumr[p][64:96, :], cum3[p][64:96, :], ALU.subtract).then_inc(V.sig(p, "ct4"), 1)

            def s_ktok(it, p):
                ve.wait_ge(M.sem[p], M.at("ktok", it))
                ve.wait_ge(S.sem[p], S.at("etok", it))
                keys = bank(p, 3).rearrange("p (ch k) -> p ch k", k=LK)
                for i, (dst, name) in enumerate(((kf[p], "kf"), (kb[p], "kb"))):
                    fade = etok[p][:, 1 - i].rearrange("p c (h a) -> p (c h) a", a=1).broadcast_to([P, CH * LH, LK])
                    ve.tensor_tensor(dst[:].rearrange("p c h k -> p (c h) k"), keys, fade, ALU.mult).then_inc(V.sig(p, name), 1)

            def s_states(it, p):
                def flat(ap):
                    return ap.rearrange("p h w -> p (h w)")
                half = LH * LW
                e = [e1t[p][:, c * P + P - 1:c * P + P] for c in range(CH)]
                ve.wait_ge(M.sem[p], M.at("F01", it))
                ve.tensor_copy(flat(st[p][:, 0]), bank(p, 0)[:, 0:half]).then_inc(V.sig(p, "s1"), 1)
                ve.wait_ge(M.sem[p], M.at("F2G3", it))
                ve.tensor_copy(flat(st[p][:, 5]), bank(p, 1)[:, half:2 * half]).then_inc(V.sig(p, "r2"), 1)
                ve.wait_ge(V.sem[p], V.at("s1", it))
                ve.scalar_tensor_tensor(flat(st[p][:, 1]), flat(st[p][:, 0]), e[1], bank(p, 0)[:, half:2 * half], ALU.mult, ALU.add).then_inc(V.sig(p, "s2"), 1)
                ve.wait_ge(V.sem[p], V.at("s2", it))
                ve.scalar_tensor_tensor(flat(st[p][:, 2]), flat(st[p][:, 1]), e[2], bank(p, 1)[:, 0:half], ALU.mult, ALU.add).then_inc(V.sig(p, "s3"), 1)
                ve.wait_ge(M.sem[p], M.at("G12", it))
                ve.scalar_tensor_tensor(flat(st[p][:, 4]), flat(st[p][:, 5]), e[2], bank(p, 2)[:, half:2 * half], ALU.mult, ALU.add).then_inc(V.sig(p, "r1"), 1)
                ve.wait_ge(V.sem[p], V.at("r1", it))
                ve.scalar_tensor_tensor(flat(st[p][:, 3]), flat(st[p][:, 4]), e[1], bank(p, 2)[:, 0:half], ALU.mult, ALU.add).then_inc(V.sig(p, "r0"), 1)

            def s_mask(i):
                def go(it, p):
                    if i == 0:
                        ve.wait_ge(G.sem[p], G.at("phiq", it))
                    if i >= 2:
                        ve.wait_ge(M.sem[p], M.at(f"scores{i - 2}", it))
                    ve.tensor_scalar(qm[p][:, i % 2, :], phiq[p][:], headmask[:, i:i + 1], None, ALU.mult).then_inc(V.sig(p, f"mask{i}"), 1)
                return go

            def s_at(i):
                def go(it, p):
                    ve.wait_ge(M.sem[p], M.at(f"scores{i}", it))
                    ve.wait_ge(S.sem[p], S.at(f"dec{i}", it))
                    if i >= 2:
                        ve.wait_ge(M.sem[p], M.at(f"intra{i - 2}", it))
                    ve.tensor_tensor(at[p][:, i % 2, :], bank(p, 0), dec[p][:, i % 2, :], ALU.mult).then_inc(V.sig(p, f"at{i}"), 1)
                return go

            def s_attn(r):
                def go(it, p):
                    ve.wait_ge(M.sem[p], M.at(f"turn{r}", it))
                    turned = bank(p, 1 + r % 2).rearrange("p (c g w) -> p c g w", c=CH, g=4)
                    ve.tensor_scalar(rden[p][:], turned[:, :, :, LK:LK + 1], LION_EPS, None, ALU.max).then_inc(V.sig(p, f"floor{r}"), 1)
                    ve.wait_ge(V.sem[p], V.at(f"floor{r}", it))
                    ve.reciprocal(rden[p][:], rden[p][:]).then_inc(V.sig(p, f"inv{r}"), 1)
                    ve.wait_ge(V.sem[p], V.at(f"inv{r}", it))
                    ve.tensor_tensor(attn[p][:, :, r], turned[:, :, :, 0:LK], rden[p][:].broadcast_to([P, CH, 4, LK]), ALU.mult).then_inc(V.sig(p, f"attn{r}"), 1)
                return go

            def s_x1(it, p):
                ve.wait_ge(M.sem[p], M.at("oproj", it))
                ve.wait_ge(G.sem[p], G.at("hob", it))
                ve.tensor_tensor(h[p][:], chunked(bank(p, 0)), hob[p][:], ALU.add).then_inc(V.sig(p, "x1"), 1)
                ve.wait_ge(V.sem[p], V.at("x1", it))
                norm_steps(it, p, "ln3", h[p], hn[p], 1e-5)

            def s_y(it, p):
                ve.wait_ge(M.sem[p], M.at("f2", it))
                ve.wait_ge(G.sem[p], G.at("x1f", it))
                ve.tensor_tensor(hn[p][:], chunked(bank(p, 2)), hob[p][:], ALU.add).then_inc(V.sig(p, "y"), 1)

            ve.wait_ge(ld_const, N_CONST)
            ve.wait_ge(pads_zero, 1)
            spread = pick1[:].rearrange("p (h a) -> p h a", a=1).broadcast_to([96, LH, P])
            ve.tensor_copy(pick[:], spread).then_inc(picks_ready, 1)
            ve.wait_ge(picks_ready, 1)
            ve.tensor_scalar(unpick[:], pick[:], -1.0, None, ALU.mult).then_inc(picks_ready, 1)
            per_head = sum([([(head_time(i) + 0.5, s_mask(i + 1))] if i + 1 < LH else []) + [(head_time(i) + 3.1, s_at(i))] + ([(head_time(i) + 4.5, s_attn((i - 6) // 4))] if i >= 6 and i % 4 == 2 else []) for i in heads], [])
            run(ve, [(1.5, s_ln1), (7.0, s_ln2), (12.9, s_tq), (12.9, s_tk), (16.4, s_zb), (16.4, s_vaug), (18.7, s_ll), (23.6, s_cum), (24.8, s_ktok), (32.0, s_states), (33.7, s_mask(0))] + per_head
                + [(DONE + 6.8, s_attn(LR - 1)), (DONE + 11.1, s_x1), (DONE + 24.6, s_y)])

        @block.scalar
        def _(ac):
            def s_xnT(it, p):
                ac.wait_ge(M.sem[p], M.at("tr1", it))
                ac.activation(xnT[p][:], bank(p, 0), ACT.Identity, bias=cols[:, 1:2], scale=cols[:, 0:1]).then_inc(S.sig(p, "xnT"), 1)

            def s_phi(it, p):
                ac.wait_ge(M.sem[p], M.at("kT", it))
                ac.wait_ge(V.sem[p], V.at("tq", it))
                ac.activation(rq[p], bank(p, 1), ACT.Relu, bias=cols[:, 4:5]).then_inc(S.sig(p, "rq"), 1)
                ac.wait_ge(V.sem[p], V.at("tk", it))
                ac.activation(rk[p], bank(p, 2), ACT.Relu, bias=cols[:, 5:6]).then_inc(S.sig(p, "rk"), 1)
                ac.activation(tq[p], tq[p], ACT.Exp).then_inc(S.sig(p, "eq"), 1)
                ac.activation(tk[p], tk[p], ACT.Exp).then_inc(S.sig(p, "ek"), 1)

            def s_decay(it, p):
                ac.wait_ge(V.sem[p], V.at("zb", it))
                ac.activation(ez[p][:], zb[p][:], ACT.Exp, scale=-1.0).then_inc(S.sig(p, "ez"), 1)
                ac.wait_ge(S.sem[p], S.at("ez", it))
                ac.activation(lnz[p][:], ez[p][:], ACT.Ln, bias=1.0).then_inc(S.sig(p, "lnz"), 1)

            def s_fades(it, p):
                ac.wait_ge(M.sem[p], M.at("ce1", it))
                ac.activation(e1t[p][:], bank(p, 0), ACT.Exp).then_inc(S.sig(p, "e1t"), 1)
                ac.wait_ge(M.sem[p], M.at("ce2", it))
                ac.activation(e2t[p][:], bank(p, 1), ACT.Exp).then_inc(S.sig(p, "e2t"), 1)
                ac.wait_ge(M.sem[p], M.at("tok", it))
                ac.activation(etok[p][:].rearrange("p a c h -> p (a c h)"), bank(p, 2)[:, 0:2 * CH * LH], ACT.Exp).then_inc(S.sig(p, "etok"), 1)

            def s_head(i):
                def go(it, p):
                    ac.wait_ge(M.sem[p], M.at(f"diff{i}", it))
                    ac.activation(absd[p][:, i % 2, :], bank(p, 3), ACT.Abs).then_inc(S.sig(p, f"abs{i}"), 1)
                    ac.wait_ge(S.sem[p], S.at(f"abs{i}", it))
                    if i >= 2:
                        ac.wait_ge(V.sem[p], V.at(f"at{i - 2}", it))
                    ac.activation(dec[p][:, i % 2, :], absd[p][:, i % 2, :], ACT.Exp, scale=-1.0).then_inc(S.sig(p, f"dec{i}"), 1)
                return go

            def s_un(r):
                def go(it, p):
                    ac.wait_ge(M.sem[p], M.at(f"intra{4 * r + 3}", it))
                    if r:
                        ac.wait_ge(M.sem[p], M.at(f"turn{r - 1}", it))
                    ac.activation(un[p][:], bank(p, 1 + r % 2), ACT.Copy).then_inc(S.sig(p, f"un{r}"), 1)
                return go

            def s_attnT(it, p):
                ac.wait_ge(M.sem[p], M.at("back", it))
                ac.activation(attnT[p][:], bank(p, 3), ACT.Copy).then_inc(S.sig(p, "attnT"), 1)

            def s_xn2T(it, p):
                ac.wait_ge(M.sem[p], M.at("tr2", it))
                ac.activation(xnT[p][:], bank(p, 1), ACT.Identity, bias=cols[:, 3:4], scale=cols[:, 2:3]).then_inc(S.sig(p, "xn2T"), 1)

            def s_gelu(m):
                def go(it, p):
                    ac.wait_ge(M.sem[p], M.at(f"f1_{m}", it))
                    ac.activation(hidden[p][:, m, :], bank(p, (2 + m) % 4), ACT.Gelu, bias=f1b[:, m:m + 1]).then_inc(S.sig(p, f"gelu{m}"), 1)
                return go

            ac.wait_ge(ld_const, N_CONST)
            run(ac, [(13.3, s_xnT), (13.3, s_phi), (20.9, s_decay), (23.1, s_fades)]
                + sum([([(head_time(i) + 3.1, s_un((i - 5) // 4))] if i >= 5 and i % 4 == 1 else []) + [(head_time(i) - 1.2, s_head(i))] for i in heads], [])
                + [(DONE + 1.6, s_un(LR - 1)), (DONE + 6.1, s_attnT), (DONE + 10.9, s_xn2T), *((DONE + (14.9, 14.9, 14.9, 14.9)[m], s_gelu(m)) for m in range(FC))])

        @block.tensor
        def _(pe):
            def transposes(dst, src):
                for c in range(CH):
                    ins = pe.transpose(dst[:, c * P:(c + 1) * P], src[:, c * P:(c + 1) * P], ident[:])
                return ins

            def s_tr1(it, p):
                pe.wait_ge(S.sem[p], S.all(it))
                pe.wait_ge(V.sem[p], V.at("ln2out", it))
                transposes(bank(p, 0), hn[p][:].rearrange("p c n -> p (c n)")).then_inc(M.sig(p, "tr1"), 1)

            def s_proj(it, p):
                pe.wait_ge(S.sem[p], S.at("xnT", it))
                pe.matmul(bank(p, 1), qw[:], xnT[p][:], start=True, stop=True).then_inc(M.sig(p, "qT"), 1)
                pe.matmul(bank(p, 2), kw[:], xnT[p][:], start=True, stop=True).then_inc(M.sig(p, "kT"), 1)
                for c in range(CH):
                    ins = pe.matmul(bank(p, 3)[:, c * LH:(c + 1) * LH], xnT[p][:, c * P:(c + 1) * P], decw[:], start=True, stop=True)
                ins.then_inc(M.sig(p, "dec"), 1)
                for c in range(CH):
                    ins = pe.matmul(bank(p, 0)[:, c * D:(c + 1) * D], xnT[p][:, c * P:(c + 1) * P], vw[:], start=True, stop=True)
                ins.then_inc(M.sig(p, "v"), 1)

            def s_cum(it, p):
                pe.wait_ge(V.sem[p], V.at("ll3", it))
                for c in range(CH):
                    ins = pe.matmul(bank(p, 3)[0:96, c * P:(c + 1) * P], ll3[p][:, c].rearrange("p a h -> p (a h)"), upto[:], start=True, stop=True)
                ins.then_inc(M.sig(p, "ct"), 1)
                pe.wait_ge(V.sem[p], V.at("llrep", it))
                for n, tri, name in ((0, upto, "ce1"), (1, after, "ce2")):
                    if n == 1:
                        pe.wait_ge(S.sem[p], S.at("rk", it))
                    for c in range(CH):
                        ins = pe.matmul(bank(p, n)[:, c * P:(c + 1) * P], llrep[p][:, c].rearrange("p h k -> p (h k)"), tri[:], start=True, stop=True)
                    ins.then_inc(M.sig(p, name), 1)
                for n, tri in ((0, upto), (1, after)):
                    ins = pe.matmul(bank(p, 2)[:, n * CH * LH:(n + 1) * CH * LH], tri[:], ll[p][:].rearrange("p c h -> p (c h)"), start=True, stop=True)
                ins.then_inc(M.sig(p, "tok"), 1)

            def s_ktok(it, p):
                pe.wait_ge(V.sem[p], V.at("ct4", it))
                pe.wait_ge(G.sem[p], G.at("phik", it))
                transposes(bank(p, 3), phik[p][:]).then_inc(M.sig(p, "ktok"), 1)

            def s_sums(it, p):
                half = LH * LW

                def one(dst, keys, c):
                    return pe.matmul(dst, keys[:, c].rearrange("p h k -> p (h k)"),
                                     vaug[p][:, c, 0:LH, :].rearrange("p h w -> p (h w)"), start=True, stop=True)
                pe.wait_ge(V.sem[p], V.at("kb", it))
                pe.wait_ge(S.sem[p], S.at("etok", it))
                one(bank(p, 0)[:, 0:half], kf[p], 0)
                one(bank(p, 0)[:, half:2 * half], kf[p], 1).then_inc(M.sig(p, "F01"), 1)
                one(bank(p, 1)[:, 0:half], kf[p], 2)
                one(bank(p, 1)[:, half:2 * half], kb[p], 3).then_inc(M.sig(p, "F2G3"), 1)
                one(bank(p, 2)[:, 0:half], kb[p], 1)
                one(bank(p, 2)[:, half:2 * half], kb[p], 2).then_inc(M.sig(p, "G12"), 1)

            def diff(it, p, i):
                pe.wait_ge(S.sem[p], S.at(f"abs{i - 1}" if i else "etok", it))
                for c in range(CH):
                    cs = slice(c * P, (c + 1) * P)
                    pe.matmul(bank(p, 3)[:, cs], pick[:, i, :], cum3[p][:, cs], start=True, stop=False, skip_group_check=True)
                    ins = pe.matmul(bank(p, 3)[:, cs], cum3[p][:, cs], unpick[:, i, :], start=False, stop=True, skip_group_check=True)
                ins.then_inc(M.sig(p, f"diff{i}"), 1)

            def scores(it, p, i):
                pe.wait_ge(V.sem[p], V.at(f"at{i - 1}" if i else "r0", it))
                pe.wait_ge(V.sem[p], V.at(f"mask{i}", it))
                for c in range(CH):
                    cs = slice(c * P, (c + 1) * P)
                    ins = pe.matmul(bank(p, 0)[:, cs], phik[p][:, cs], qm[p][:, i % 2, cs], start=True, stop=True)
                ins.then_inc(M.sig(p, f"scores{i}"), 1)

            def inter(it, p, r):
                pe.wait_ge(G.sem[p], G.at("sp5", it))
                pe.wait_ge(V.sem[p], V.at(f"attn{r - 2}" if r >= 2 else "r0", it))
                first = True
                for c in range(CH):
                    cs = slice(c * P, (c + 1) * P)
                    for n, q in ([(c - 1, qf[p])] if c else []) + ([(3 + c, qb[p])] if c < CH - 1 else []):
                        ins = pe.matmul(bank(p, 1 + r % 2)[:, cs], stp[p][:, n, r].rearrange("p g w -> p (g w)"), q[:, cs],
                                        start=first, stop=False, skip_group_check=True)
                        first = False
                ins.then_inc(M.sig(p, f"inter{r}"), 1)

            def intra(it, p, i):
                g = i % 4
                pe.wait_ge(V.sem[p], V.at(f"at{i}", it))
                for c in range(CH):
                    cs = slice(c * P, (c + 1) * P)
                    ins = pe.matmul(bank(p, 1 + i // 4 % 2)[32 * g:32 * g + 32, cs], vaug[p][:, c, i:i + 2, :].rearrange("p h w -> p (h w)"),
                                    at[p][:, i % 2, cs], start=False, stop=True, skip_group_check=True)
                ins.then_inc(M.sig(p, f"intra{i}"), 1)

            def turn(it, p, r):
                pe.wait_ge(S.sem[p], S.at(f"un{r}", it))
                transposes(bank(p, 1 + r % 2), un[p][:]).then_inc(M.sig(p, f"turn{r}"), 1)

            def at_step(step, i):
                def go(it, p):
                    step(it, p, i)
                return go

            def s_back(it, p):
                pe.wait_ge(V.sem[p], V.at(f"attn{LR - 1}", it))
                pe.wait_ge(S.sem[p], S.at(f"dec{LH - 1}", it))
                transposes(bank(p, 3), attn[p][:].rearrange("p c r g k -> p (c r g k)")).then_inc(M.sig(p, "back"), 1)

            def s_oproj(it, p):
                pe.wait_ge(S.sem[p], S.at("attnT", it))
                for c in range(CH):
                    ins = pe.matmul(bank(p, 0)[:, c * D:(c + 1) * D], attnT[p][:, c * P:(c + 1) * P], ow[:], start=True, stop=True)
                ins.then_inc(M.sig(p, "oproj"), 1)

            def s_tr2(it, p):
                pe.wait_ge(V.sem[p], V.at("ln3out", it))
                transposes(bank(p, 1), hn[p][:].rearrange("p c n -> p (c n)")).then_inc(M.sig(p, "tr2"), 1)

            def f1(it, p, m):
                if m == 0:
                    pe.wait_ge(S.sem[p], S.at("xn2T", it))
                pe.matmul(bank(p, (2 + m) % 4), f1w[:, m * P:(m + 1) * P], xnT[p][:], start=True, stop=True).then_inc(M.sig(p, f"f1_{m}"), 1)

            def f2(it, p, c):
                if c == 0:
                    pe.wait_ge(S.sem[p], S.at(f"gelu{FC - 1}", it))
                for m in range(FC):
                    ins = pe.matmul(bank(p, 2)[:, c * D:(c + 1) * D], hidden[p][:, m, c * P:(c + 1) * P], f2w[:, m, :],
                                    start=(m == 0), stop=(m == FC - 1))
                if c == CH - 1:
                    ins.then_inc(M.sig(p, "f2"), 1)

            pe.wait_ge(ld_const, N_CONST)
            pe.wait_ge(picks_ready, 2)
            def head_steps(i):
                steps = [(-2.2, diff, i), (0.2, scores, i)]
                if i:
                    steps += [(1.7, intra, i - 1)]
                if i % 4 == 0:
                    steps += [(3.3, inter, i // 4)]
                if i >= 6 and i % 4 == 2:
                    steps += [(-0.1, turn, (i - 6) // 4)]
                return [(head_time(i) + after, at_step(step, n)) for after, step, n in steps]

            run(pe, [(9.2, s_tr1), (9.2, s_proj), (20.4, s_cum), (25.0, s_ktok), (25.9, s_sums)]
                + sum([head_steps(i) for i in heads], [])
                + [(DONE + 0.1, at_step(intra, LH - 1)), (DONE + 0.1, at_step(turn, LR - 1)), (DONE + 5.4, s_back), (DONE + 5.4, s_oproj), (DONE + 13.5, s_tr2)]
                + [(DONE + (16.8, 16.8, 16.8, 16.8)[m], at_step(f1, m)) for m in range(FC)] + [(DONE + (21.7, 21.7, 21.7, 21.7)[c], at_step(f2, c)) for c in range(CH)])


class Count:

    AHEAD = 4

    def __init__(self, sem, events, slots, by=1):
        self.sem, self.events, self.slots, self.by = sem, events, slots, by

    def start(self, eng):
        eng.sem_inc(self.sem, self.AHEAD * self.events * self.by)

    def at(self, it, s, k=0):
        return it * (self.slots * self.events * self.by) + ((s + self.AHEAD) * self.events + k + 1) * self.by


def chain_weights(nc, a, w):
    ctx = ExitStack()
    with ctx:
        def sb(name, shape, dt=FP32):
            return ctx.enter_context(nc.sbuf_tensor("w_" + name, shape, dt))

        ident = sb("ident", [P, P])
        ew, aw = sb("ew", [P, NODES, 3]), sb("aw", [P, NODES])
        beT = sb("beT", [P, 20])
        edge = sb("edge", [P, 2, NODES, D])
        edgeT = sb("edgeT", [P, 2, NODES, D])
        wkv = sb("wkv", [P, 2, NODES, D])
        wo = sb("wo", [P, NODES, D])
        edge_q = sb("wq", [P, NODES, D])
        wkd = sb("wkd", [P, NODES, D])
        bv = sb("bv", [P, NODES])
        ps = ctx.enter_context(nc.psum_tensor("w_ps", [P, 8, 512], FP32))
        loaded = ctx.enter_context(nc.semaphore("w_loaded"))
        sem = [[ctx.enter_context(nc.semaphore("w_" + n))] for n in ("tensor_steps", "vector_steps")]
        M = Steps(sem[0], ["turned", "joined", "biases", "bo"])
        V = Steps(sem[1], ["ordered", "turned", "joined", "biases", "wo", "bo"])
        block = ctx.enter_context(nc.Block())
        n_loads = [0]

        @block.sync
        def _(sync):
            def load(dst, src):
                n_loads[0] += 16
                sync.dma_start(dst, src, allow_slow_non_contiguous=True).then_inc(loaded, 16)

            load(ident[:], a["c_ident"])
            load(beT[:], a["be"].rearrange("e d -> d e"))
            load(ew[:], a["ew"].rearrange("(x c) k -> x c k", x=1).broadcast_to([P, NODES, 3]))
            load(aw[:], a["act_w"].rearrange("(x c) -> x c", x=1).broadcast_to([P, NODES]))
            load(edge_q[:], a["Wq"].rearrange("c m n -> m c n"))
            load(wkv[:, 0], a["Wk"].rearrange("c m n -> m c n"))
            load(wkv[:, 1], a["Wv"].rearrange("c m n -> m c n"))
            load(wo[:], a["Wo"].rearrange("c m n -> m c n"))
            for c, (edges, _) in enumerate(WIRING):
                load(w["wqe"][:, c, :], a["We"][edges[0]])
                load(edge[:, 0, c, :], a["We"][edges[1]])
                load(edge[:, 1, c, :], a["We"][edges[2]])
            M.start(sync)
            V.start(sync)
            sync.wait_ge(loaded, n_loads[0])

        ALL = 16 * (8 + 3 * NODES)

        @block.tensor
        def _(pe):
            pe.wait_ge(loaded, ALL)
            for k in range(2):
                for c in range(NODES):
                    n = k * NODES + c
                    ins = pe.transpose(ps[:, n // 4, (n % 4) * P:(n % 4 + 1) * P], edge[:, k, c, :], ident[:])
            ins.then_inc(M.sig(0, "turned"), 1)
            pe.wait_ge(V.sem[0], V.at("turned", 0))
            heads = [wkd[:], wkv[:, 1]]
            for k in range(2):
                for c in range(NODES):
                    n = k * NODES + c
                    ins = pe.matmul(ps[:, 3 + n // 4, (n % 4) * P:(n % 4 + 1) * P], edgeT[:, k, c, :], heads[k][:, c, :], start=True, stop=True)
            ins.then_inc(M.sig(0, "joined"), 1)
            for k in range(2):
                for c, (edges, _) in enumerate(WIRING):
                    e = edges[1 + k]
                    ins = pe.matmul(ps[:, 6, k * NODES + c:k * NODES + c + 1], heads[k][:, c, :], beT[:, e:e + 1], start=True, stop=True)
            ins.then_inc(M.sig(0, "biases"), 1)
            pe.wait_ge(V.sem[0], V.at("wo", 0))
            for c in range(NODES):
                ins = pe.matmul(ps[:, 7, c:c + 1], w["wo"][:, c, :], bv[:, c:c + 1], start=True, stop=True)
            ins.then_inc(M.sig(0, "bo"), 1)

        @block.vector
        def _(ve):
            ve.wait_ge(loaded, ALL)
            for c in range(NODES):
                for dst, src in ((w["wq"], edge_q), (wkd, wkv[:, 0])):
                    ins = ve.tensor_copy(dst[:, c, :].rearrange("p (d h) -> p d h", h=MH), src[:, c, :].rearrange("p (h d) -> p d h", h=MH))
            ins.then_inc(V.sig(0, "ordered"), 1)
            ve.wait_ge(M.sem[0], M.at("turned", 0))
            ve.tensor_copy(edgeT[:].rearrange("p k c n -> p (k c n)"), ps[:, 0:3, :].rearrange("p a n -> p (a n)")).then_inc(V.sig(0, "turned"), 1)
            ve.wait_ge(M.sem[0], M.at("joined", 0))
            for k in range(2):
                for c in range(NODES):
                    n = k * NODES + c
                    ins = ve.tensor_scalar((w["wk"], w["wv"])[k][:, c, :], ps[:, 3 + n // 4, (n % 4) * P:(n % 4 + 1) * P],
                                           ew[:, c, 1 + k:2 + k], None, ALU.mult)
            ins.then_inc(V.sig(0, "joined"), 1)
            ve.wait_ge(M.sem[0], M.at("biases", 0))
            ve.tensor_tensor(w["bk"][:], ps[:, 6, 0:NODES], ew[:, :, 1], ALU.mult)
            for c, (edges, _) in enumerate(WIRING):
                ve.tensor_scalar(w["bq"][:, c:c + 1], beT[:, edges[0]:edges[0] + 1], ew[:, c, 0:1], None, ALU.mult)
                ve.tensor_copy(w["eq"][:, c:c + 1], ew[:, c, 0:1])
            ve.tensor_tensor(bv[:], ps[:, 6, NODES:2 * NODES], ew[:, :, 2], ALU.mult).then_inc(V.sig(0, "biases"), 1)
            for c in range(NODES):
                ins = ve.tensor_scalar(w["wo"][:, c, :], wo[:, c, :], aw[:, c:c + 1], None, ALU.mult)
            ins.then_inc(V.sig(0, "wo"), 1)
            ve.wait_ge(M.sem[0], M.at("bo", 0))
            ve.tensor_copy(w["bo"][:], ps[:, 7, 0:NODES]).then_inc(V.sig(0, "bo"), 1)


LANES = 4
SLOTS = NODES * LANES
TILE = {-1: 0, 0: 1, 1: 2, 2: 3, 3: 4, 4: 0, 5: 2}
RING = 4
PRING = 3
SCALE = DH ** -0.5


def node_chain_phase(nc, a, w, mod_rows, x_mid, out):
    ctx = ExitStack()
    with ctx:
        def sb(name, shape, dt=FP32):
            return ctx.enter_context(nc.sbuf_tensor("b_" + name, shape, dt))

        counts = []

        def count(name, events, slots=SLOTS, by=1):
            counts.append(Count(ctx.enter_context(nc.semaphore("b_" + name)), events, slots, by))
            return counts[-1]

        ident, identb = sb("ident", [P, P]), sb("identb", [P, P], BF16)
        gain, shift = sb("gain", [P, 1, D]), sb("shift", [P, 1, D])
        minus_half, zero, spare = sb("minus_half", [P, CH, 1]), sb("zero", [P, 1]), sb("spare", [P, 1])
        xi = [sb(f"xi{n}", [P, CH, D]) for n in range(2)]
        modi = [sb(f"modi{n}", [P, 2, D]) for n in range(2)]
        xo = [sb(f"xo{n}", [P, CH, D]) for n in range(2)]
        gate = [sb(f"gate{n}", [P, 1, D]) for n in range(2)]
        gated = sb("gated", [P, 2, D])
        node = [[sb(f"node{n}_{i}", [P, T]) for i in range(5)] for n in range(LANES)]
        stats, mv, var, rstd = sb("stats", [P, CH, 6]), sb("mv", [P, CH, 2]), sb("var", [P, CH, 1]), sb("rstd", [P, CH, 1])
        hx = [sb(f"hx{n}", [P, CH, D]) for n in range(2)]
        qf, kf, rest = sb("qf", [P, T]), sb("kf", [P, T]), sb("rest", [P, T])
        qp, kp = ([sb(f"{n}{i}", [P, 3, T], BF16) for i in range(2)] for n in ("qp", "kp"))
        qst, kst = ([sb(f"{n}{i}", [SROWS + 2, MH, T], BF16) for i in range(RING)] for n in ("qst", "kst"))
        vaug = [sb(f"vaug{i}", [P, CH, MH, 2 * DH]) for i in range(RING)]
        mx = [sb(f"mx{i}", [P, MH, CH]) for i in range(2)]
        nm = [sb(f"nm{g}", [P, CH, 2, 4], BF16) for g in range(MG)]
        nrow = [sb(f"nrow{g}", [8, T], BF16) for g in range(MG)]
        prob = [sb(f"prob{i}", [P, 4, T]) for i in range(PRING)]
        ctxu = [sb(f"ctxu{g}", [P, T]) for g in range(MG)]
        rden = sb("rden", [P, CH, 4, 1])
        ctxn, ctxT = sb("ctxn", [P, CH, D]), sb("ctxT", [P, T])
        ps = ctx.enter_context(nc.psum_tensor("b_ps", [P, 8, T], FP32))
        s1_bank = [ps[:, n, :] for n in range(2)]
        s2_bank = [ps[:, 2 + 2 * n:4 + 2 * n, :] for n in range(2)]
        ctx_bank, misc = ps[:, 6, :], ps[:, 7, :]

        loaded = ctx.enter_context(nc.semaphore("b_const_loaded"))
        ones_ready = ctx.enter_context(nc.semaphore("b_ones_ready"))
        filled = ctx.enter_context(nc.semaphore("b_filled"))
        x_in, x_again, stored = ([count(f"{n}{i}", 1, LANES // 2, by) for i in range(2)]
                                 for n, by in (("x_in", 32), ("x_again", 32), ("stored", 16)))
        h_stats, h_aggr, h_eps, h_out = (count(n, 1, LANES) for n in ("h_stats", "h_aggr", "h_eps", "h_out"))
        h_rstd, h_scaled, h_ready, h_turned, n0_ready = (count(n, 1, LANES) for n in
                                                         ("h_rstd", "h_scaled", "h_ready", "h_turned", "n0_ready"))
        o_turned, o_copied, o_stats, o_aggr, o_eps, o_norm = (count(n, 1, LANES) for n in ("o_turned", "o_copied", "o_stats", "o_aggr", "o_eps", "o_norm"))
        o_rstd, o_gain, o_scaled, o_ready = (count(n, e, LANES) for n, e in (("o_rstd", 1), ("o_gain", 1), ("o_scaled", 2), ("o_ready", 1)))
        k_raw, q_raw, qq_raw, v_raw = (count(n, 1) for n in ("k_raw", "q_raw", "qq_raw", "v_raw"))
        k_ready, q_ready, qq_ready, v_ready = (count(n, 1) for n in ("k_ready", "q_ready", "qq_ready", "v_ready"))
        k_split, q_split = count("k_split", 4), count("q_split", 4)
        k_stacked, q_stacked = ([count(f"{n}{i}", PARTS, SLOTS // 2, 16) for i in range(2)] for n in ("k_stacked", "q_stacked"))
        s1_done, max_done = count("s1_done", MH * CH), count("max_done", MH * CH)
        max_split, max_turned, max_row = count("max_split", 2 * MG), count("max_turned", MG), count("max_row", MG)
        max_stacked = [count(f"max_stacked{g}", 1, by=16) for g in range(MG)]
        UNITS = MG * CH
        s2_done, exp_done, pv_done = count("s2_done", 2 * UNITS), count("exp_done", 2 * UNITS), count("pv_done", UNITS)
        ctx_out, ctx_turned, den_inv, ctx_norm = (count(n, MG) for n in ("ctx_out", "ctx_turned", "den_inv", "ctx_norm"))
        ctx_back, ctxT_ready, o_raw, node_ready = (count(n, 1) for n in ("ctx_back", "ctxT_ready", "o_raw", "node_ready"))
        N_CONST = 16 * 3
        block = ctx.enter_context(nc.Block())

        def lane(s):
            return s % LANES

        def node_of(s):
            return s // LANES % NODES

        def tile(s, n):
            return node[lane(s)][TILE[n]]

        def last_node(s):
            return node_of(s) == NODES - 1

        def wait_node(eng, it, s, n):
            group = s // SLOTS
            if n < 0:
                eng.wait_ge(n0_ready.sem, n0_ready.at(it, group * LANES + lane(s)))
            else:
                eng.wait_ge(node_ready.sem, node_ready.at(it, group * SLOTS + n * LANES + lane(s)))

        INPUT = SLOTS - LANES - 2

        def run(eng, inputs, time):
            for n in range(LANES):
                inputs(0, n)
            for t in range(-3, 1):
                time(0, t, lambda s: s >= 0)
            with eng.Fori(0, B // LANES - 1) as it:
                for t in range(1, SLOTS + 1):
                    time(it, t, lambda s: True)
            for t in range(1, SLOTS + 1):
                time(B // LANES - 1, t, lambda s: s < SLOTS)

        @block.sync
        def _(sync):
            sync.dma_start(ident[:], a["c_ident"]).then_inc(loaded, 16)
            sync.dma_start(gain[:, 0, :], a["ln_g"].rearrange("(a n) -> a n", a=1).broadcast_to([P, D])).then_inc(loaded, 16)
            sync.dma_start(shift[:, 0, :], a["ln_b"].rearrange("(a n) -> a n", a=1).broadcast_to([P, D])).then_inc(loaded, 16)
            for c in counts:
                c.start(sync)

            def stack(it, s, parts, order, split, dst, done):
                sync.wait_ge(split.sem, split.at(it, s, 3))
                for i, part in enumerate(order):
                    src = parts[s % 2][:, part, :]
                    sync.dma_start(dst[s % RING][i * DH:(i + 1) * DH], src).then_inc(done[s % 2].sem, 16)

            def store_max(it, s, g):
                sync.wait_ge(max_row.sem, max_row.at(it, s, g))
                for_h = qst[s % RING][SROWS:SROWS + 2, 4 * g:4 * g + 4, :]
                sync.dma_start(for_h, nrow[g][:]).then_inc(max_stacked[g].sem, 16)

            def load(it, n):
                b = sync.snap(it * LANES + n) if n >= LANES or not isinstance(it, int) else n
                sync.wait_ge(h_turned.sem, h_turned.at(it, n - 2))
                sync.dma_start(xi[n % 2][:], x_mid[bass.ds(b, 1)].rearrange("a (c p) n -> (a p) c n", p=P)).then_inc(x_in[n % 2].sem, 16)
                sync.dma_start(modi[n % 2][:], mod_rows[bass.ds(b, 1), 3 * D:5 * D].rearrange("a (k n) -> a k n", k=2).broadcast_to([P, 2, D])).then_inc(x_in[n % 2].sem, 16)

            def load_again(it, n):
                b = it * LANES + n if isinstance(it, int) else sync.snap(it * LANES + n)
                sync.wait_ge(o_ready.sem, o_ready.at(it, n - 2))
                sync.dma_start(xo[n % 2][:], x_mid[bass.ds(b, 1)].rearrange("a (c p) n -> (a p) c n", p=P)).then_inc(x_again[n % 2].sem, 16)
                sync.dma_start(gate[n % 2][:], mod_rows[bass.ds(b, 1), 5 * D:6 * D].rearrange("a (k n) -> a k n", k=1).broadcast_to([P, 1, D])).then_inc(x_again[n % 2].sem, 16)

            def store(it, n):
                b = it * LANES + n if isinstance(it, int) else sync.snap(it * LANES + n)
                sync.wait_ge(o_ready.sem, o_ready.at(it, n))
                sync.dma_start(out[bass.ds(b, 1)].rearrange("a (c p) n -> (a p) c n", p=P), hx[n % 2][:]).then_inc(stored[n % 2].sem, 16)

            def time(it, t, valid):
                if INPUT <= t < INPUT + LANES and valid(SLOTS):
                    load(it, LANES + t - INPUT)
                if valid(t):
                    store_max(it, t, 1)
                if valid(t + 2):
                    stack(it, t + 2, kp, K_PART, k_split, kst, k_stacked)
                    stack(it, t + 2, qp, Q_PART, q_split, qst, q_stacked)
                if valid(t + 1):
                    store_max(it, t + 1, 0)
                if t >= 1 and last_node(t - 1):
                    load_again(it, lane(t - 1))
                    store(it, lane(t - 1))

            run(sync, load, time)
            for n in range(2):
                sync.wait_ge(stored[n].sem, stored[n].at(B // LANES, -1))

        @block.gpsimd
        def _(gp):
            gp.memset(minus_half[:], -0.5)
            for i in range(RING):
                gp.memset(vaug[i][:], 1.0)
            gp.memset(zero[:], 0.0).then_inc(filled, 1)
            gp.wait_ge(filled, 1)
            gp.wait_ge(loaded, N_CONST)
            gp.tensor_copy(identb[:], ident[:]).then_inc(filled, 1)
            rows = [P, CH, D]

            def input_norm(it, n):
                gp.wait_ge(h_eps.sem, h_eps.at(it, n))
                gp.tensor_tensor(rstd[:], var[:], minus_half[:], ALU.pow).then_inc(h_rstd.sem, 1)
                gp.wait_ge(h_out.sem, h_out.at(it, n))
                gp.tensor_tensor(xi[n % 2][:], xi[n % 2][:], modi[n % 2][:, 1:2, :].broadcast_to(rows), ALU.mult).then_inc(h_scaled.sem, 1)
                gp.wait_ge(h_scaled.sem, h_scaled.at(it, n))
                gp.tensor_tensor(xi[n % 2][:], xi[n % 2][:], modi[n % 2][:, 0:1, :].broadcast_to(rows), ALU.add).then_inc(h_ready.sem, 1)

            def split(it, s, ready, whole, parts, stacked, done, before):
                gp.wait_ge(ready.sem, ready.at(it, s))
                gp.wait_ge(stacked[s % 2].sem, stacked[s % 2].at(it, (s - 2) // 2, PARTS - 1))
                p = parts[s % 2]
                z = zero[:].broadcast_to([P, T])
                gp.tensor_tensor(p[:, 0, :], whole[:], z, ALU.add).then_inc(done.sem, 1)
                gp.wait_ge(done.sem, done.at(it, s, 0))
                gp.wait_ge(before[0].sem, before[0].at(it, before[1], 3))
                gp.tensor_tensor(rest[:], whole[:], p[:, 0, :], ALU.subtract).then_inc(done.sem, 1)
                gp.wait_ge(done.sem, done.at(it, s, 1))
                gp.tensor_tensor(p[:, 1, :], rest[:], z, ALU.add).then_inc(done.sem, 1)
                gp.wait_ge(done.sem, done.at(it, s, 2))
                gp.wait_ge(s2_done.sem, s2_done.at(it, s - RING, 2 * UNITS - 1))
                gp.tensor_tensor(p[:, 2, :], rest[:], p[:, 1, :], ALU.subtract).then_inc(done.sem, 1)

            def output(it, s):
                n = lane(s)
                gp.wait_ge(o_eps.sem, o_eps.at(it, n))
                gp.tensor_tensor(rstd[:], var[:], minus_half[:], ALU.pow).then_inc(o_rstd.sem, 1)
                gp.wait_ge(x_again[n % 2].sem, x_again[n % 2].at(it, n // 2))
                gp.wait_ge(o_scaled.sem, o_scaled.at(it, n - 1, 1))
                gp.tensor_tensor(gated[:, 0:1, :], gate[n % 2][:], gain[:], ALU.mult)
                gp.tensor_tensor(gated[:, 1:2, :], gate[n % 2][:], shift[:], ALU.mult).then_inc(o_gain.sem, 1)
                gp.wait_ge(o_gain.sem, o_gain.at(it, n))
                gp.tensor_tensor(xo[n % 2][:], xo[n % 2][:], gated[:, 1:2, :].broadcast_to(rows), ALU.add).then_inc(o_scaled.sem, 1)
                gp.wait_ge(o_norm.sem, o_norm.at(it, n))
                gp.tensor_tensor(hx[n % 2][:], hx[n % 2][:], gated[:, 0:1, :].broadcast_to(rows), ALU.mult).then_inc(o_scaled.sem, 1)
                gp.wait_ge(o_scaled.sem, o_scaled.at(it, n, 1))
                gp.tensor_tensor(hx[n % 2][:], hx[n % 2][:], xo[n % 2][:], ALU.add).then_inc(o_ready.sem, 1)

            def time(it, t, valid):
                if valid(t + 3):
                    split(it, t + 3, k_ready, kf, kp, k_stacked, k_split, (q_split, t + 2))
                if INPUT <= t < INPUT + LANES and valid(SLOTS):
                    input_norm(it, LANES + t - INPUT)
                if t >= 1 and last_node(t - 1):
                    output(it, t - 1)
                if valid(t + 3):
                    split(it, t + 3, qq_ready, qf, qp, q_stacked, q_split, (k_split, t + 3))

            run(gp, input_norm, time)

        @block.vector
        def _(ve):
            for i in range(RING):
                ins = ve.memset(kst[i][SROWS:SROWS + 2], 1.0)
            ins.then_inc(ones_ready, 1)
            ve.wait_ge(loaded, N_CONST)
            ve.wait_ge(filled, 1)

            def norm(it, n, src, dst, eps, stats_c, aggr_c, eps_c, rstd_c, out_c):
                for c in range(CH):
                    ins = ve.bn_stats(stats[:, c, :], src[:, c, :])
                ins.then_inc(stats_c.sem, 1)
                ve.wait_ge(stats_c.sem, stats_c.at(it, n))
                ve.memset(spare[:], 0.0)
                for c in range(CH):
                    ins = ve.bn_aggr(mv[:, c, :], stats[:, c, :])
                ins.then_inc(aggr_c.sem, 1)
                ve.wait_ge(aggr_c.sem, aggr_c.at(it, n))
                ve.tensor_scalar(var[:], mv[:, :, 1:2], eps, None, ALU.add).then_inc(eps_c.sem, 1)
                ve.wait_ge(rstd_c.sem, rstd_c.at(it, n))
                for c in range(CH):
                    ins = ve.tensor_scalar(dst[:, c, :], src[:, c, :], mv[:, c, 0:1], rstd[:, c, :], ALU.subtract, ALU.mult)
                ins.then_inc(out_c.sem, 1)

            def input_norm(it, n):
                ve.wait_ge(x_in[n % 2].sem, x_in[n % 2].at(it, n // 2))
                norm(it, n, xi[n % 2], xi[n % 2], 1e-5, h_stats, h_aggr, h_eps, h_rstd, h_out)

            def maxima(it, s, half_step):
                for k in (2 * half_step, 2 * half_step + 1):
                    ve.wait_ge(s1_done.sem, s1_done.at(it, s, k))
                    ve.tensor_reduce(mx[s % 2][:, k // CH, k % CH:k % CH + 1], s1_bank[k % 2], AX.X, ALU.max).then_inc(max_done.sem, 1)

            def split_max(it, s, g):
                ve.wait_ge(max_done.sem, max_done.at(it, s, (4 * g + 4) * CH - 1))
                ve.wait_ge(max_turned.sem, max_turned.at(it, s - 1, g))
                m = mx[s % 2][:, 4 * g:4 * g + 4, :].rearrange("p h c -> p c h")
                ve.tensor_scalar(nm[g][:, :, 0, :], m, -1.0, None, ALU.mult).then_inc(max_split.sem, 1)
                ve.wait_ge(max_split.sem, max_split.at(it, s, 2 * g))
                ve.scalar_tensor_tensor(nm[g][:, :, 1, :], m, -1.0, nm[g][:, :, 0, :], ALU.mult, ALU.subtract).then_inc(max_split.sem, 1)

            def normalise(it, s, g):
                ve.wait_ge(ctx_turned.sem, ctx_turned.at(it, s, g))
                turned = misc.rearrange("p (c h w) -> p (c h) w", c=CH, h=4)
                ve.reciprocal(rden[:].rearrange("p c h w -> p (c h) w"), turned[:, :, DH:DH + 1]).then_inc(den_inv.sem, 1)
                ve.wait_ge(den_inv.sem, den_inv.at(it, s, g))
                if g == 0:
                    ve.wait_ge(ctx_back.sem, ctx_back.at(it, s - 1))
                ve.tensor_tensor(ctxn[:, :, 64 * g:64 * g + 64].rearrange("p c (h d) -> p c h d", h=4),
                                 misc.rearrange("p (c h w) -> p c h w", c=CH, h=4)[:, :, :, 0:DH],
                                 rden[:].broadcast_to([P, CH, 4, DH]), ALU.mult).then_inc(ctx_norm.sem, 1)

            def finish_node(it, s):
                ve.wait_ge(o_raw.sem, o_raw.at(it, s))
                c = node_of(s)
                x = tile(s, c)
                ve.scalar_tensor_tensor(x[:], misc, w["bo"][:, c:c + 1], x[:], ALU.add, ALU.add).then_inc(node_ready.sem, 1)

            def output(it, s):
                n = lane(s)
                ve.wait_ge(o_copied.sem, o_copied.at(it, n))
                norm(it, n, hx[n % 2], hx[n % 2], 1e-6, o_stats, o_aggr, o_eps, o_rstd, o_norm)

            def time(it, t, valid):
                for hs in range(2 * UNITS):
                    if valid(t + 1):
                        maxima(it, t + 1, hs)
                        if hs == 7:
                            split_max(it, t + 1, 0)
                        if hs == 15:
                            split_max(it, t + 1, 1)
                    if hs == 3 and INPUT <= t < INPUT + LANES and valid(SLOTS):
                        input_norm(it, LANES + t - INPUT)
                    if hs == 4 and t >= 1:
                        normalise(it, t - 1, 1)
                    if hs == 8 and t >= 1:
                        finish_node(it, t - 1)
                    if hs == 11 and t >= 1 and last_node(t - 1):
                        output(it, t - 1)
                    if hs == 13 and valid(t):
                        normalise(it, t, 0)

            run(ve, input_norm, time)

        @block.scalar
        def _(ac):
            ac.wait_ge(loaded, N_CONST)

            def first_node(it, n):
                ac.wait_ge(h_turned.sem, h_turned.at(it, n))
                ac.activation(node[lane(n)][TILE[-1]][:], misc, ACT.Copy).then_inc(n0_ready.sem, 1)

            def exps(it, s, hs):
                n = UNITS * s + hs // 2
                ac.wait_ge(s2_done.sem, s2_done.at(it, s, hs))
                if hs % 2 == 0:
                    m = n - PRING
                    ac.wait_ge(pv_done.sem, pv_done.at(it, m // UNITS, m % UNITS))
                ac.activation(prob[n % PRING][:, 2 * (hs % 2):2 * (hs % 2) + 2, :], s2_bank[hs % 2], ACT.Exp).then_inc(exp_done.sem, 1)

            def keys(it, s):
                c = node_of(s)
                ac.wait_ge(k_raw.sem, k_raw.at(it, s))
                ac.wait_ge(k_split.sem, k_split.at(it, s - 1, 3))
                ac.activation(kf[:], misc, ACT.Identity, bias=w["bk"][:, c:c + 1]).then_inc(k_ready.sem, 1)

            def node_queries(it, s):
                c = node_of(s)
                ac.wait_ge(q_raw.sem, q_raw.at(it, s))
                ac.activation(tile(s, c)[:], misc, ACT.Identity, bias=w["bq"][:, c:c + 1], scale=w["eq"][:, c:c + 1]).then_inc(q_ready.sem, 1)

            def head_queries(it, s):
                ac.wait_ge(qq_raw.sem, qq_raw.at(it, s))
                ac.wait_ge(q_split.sem, q_split.at(it, s - 1, 3))
                ac.activation(qf[:], misc, ACT.Copy, scale=SCALE).then_inc(qq_ready.sem, 1)

            def values(it, s):
                ac.wait_ge(v_raw.sem, v_raw.at(it, s))
                ac.wait_ge(pv_done.sem, pv_done.at(it, s - RING, UNITS - 1))
                ac.activation(vaug[s % RING][:, :, :, 0:DH], misc.rearrange("p (c h d) -> p c h d", c=CH, h=MH), ACT.Copy).then_inc(v_ready.sem, 1)

            def output(it, s):
                n = lane(s)
                ac.wait_ge(o_turned.sem, o_turned.at(it, n))
                ac.wait_ge(stored[n % 2].sem, stored[n % 2].at(it, n // 2 - 1))
                ac.activation(hx[n % 2][:].rearrange("p c n -> p (c n)"), misc, ACT.Copy).then_inc(o_copied.sem, 1)

            def max_rows(it, s, g):
                ac.wait_ge(max_turned.sem, max_turned.at(it, s, g))
                ac.wait_ge(max_stacked[g].sem, max_stacked[g].at(it, s - 1))
                ac.activation(nrow[g][:], misc.bitcast(BF16)[0:8, 0:T], ACT.Copy).then_inc(max_row.sem, 1)

            def context(it, s, g):
                ac.wait_ge(pv_done.sem, pv_done.at(it, s, CH * g + CH - 1))
                ac.wait_ge(ctx_turned.sem, ctx_turned.at(it, s - 1, g))
                ac.activation(ctxu[g][:], ctx_bank, ACT.Copy).then_inc(ctx_out.sem, 1)

            def context_back(it, s):
                ac.wait_ge(ctx_back.sem, ctx_back.at(it, s))
                ac.wait_ge(o_raw.sem, o_raw.at(it, s - 1))
                ac.activation(ctxT[:], misc, ACT.Copy).then_inc(ctxT_ready.sem, 1)

            def time(it, t, valid):
                for hs in range(2 * UNITS):
                    if valid(t):
                        exps(it, t, hs)
                    if hs == 1 and t >= 1:
                        context(it, t - 1, 1)
                    if hs == 1 and valid(t + 3):
                        keys(it, t + 3)
                    if hs == 2 and valid(t):
                        max_rows(it, t, 1)
                    if hs == 5 and INPUT + 1 <= t < INPUT + 1 + LANES and valid(SLOTS):
                        first_node(it, LANES + t - INPUT - 1)
                    if hs == 6 and t >= 1:
                        context_back(it, t - 1)
                    if hs == 9 and valid(t):
                        context(it, t, 0)
                    if hs == 9 and valid(t + 1):
                        max_rows(it, t + 1, 0)
                    if hs == 10 and valid(t + 3):
                        node_queries(it, t + 3)
                    if hs == 11 and t >= 1 and last_node(t - 1):
                        output(it, t - 1)
                    if hs == 12 and valid(t + 3):
                        head_queries(it, t + 3)
                    if hs == 14 and valid(t + 3):
                        values(it, t + 3)

            run(ac, first_node, time)

        @block.tensor
        def _(pe):
            pe.wait_ge(loaded, N_CONST)
            pe.wait_ge(filled, 2)
            pe.wait_ge(ones_ready, 1)
            free = [None]

            def shared(it, reader, s, k=0):
                if free[0]:
                    c, s0, k0 = free[0]
                    pe.wait_ge(c.sem, c.at(it, s0, k0))
                free[0] = (reader, s, k)

            def transposes(src):
                for c in range(CH):
                    ins = pe.transpose(misc[:, c * P:(c + 1) * P], src[:, c * P:(c + 1) * P], ident[:])
                return ins

            def first_node(it, n):
                shared(it, n0_ready, n)
                pe.wait_ge(h_ready.sem, h_ready.at(it, n))
                transposes(xi[n % 2][:].rearrange("p c n -> p (c n)")).then_inc(h_turned.sem, 1)

            def scores_by_query(it, s, hs, half):
                h, k = hs // 2, 2 * hs + half
                if k == 0:
                    pe.wait_ge(k_stacked[s % 2].sem, k_stacked[s % 2].at(it, s // 2, PARTS - 1))
                    pe.wait_ge(q_stacked[s % 2].sem, q_stacked[s % 2].at(it, s // 2, PARTS - 1))
                m = s * MH * CH + k - 2
                pe.wait_ge(max_done.sem, max_done.at(it, m // (MH * CH), m % (MH * CH)))
                c = k % CH
                pe.matmul(s1_bank[k % 2], qst[s % RING][0:SROWS, h, c * P:(c + 1) * P], kst[s % RING][0:SROWS, h, :],
                          start=True, stop=True).then_inc(s1_done.sem, 1)

            def scores_by_key(it, s, hs, half):
                u = hs // 2
                g, c = u // CH, u % CH
                if half == 0:
                    if hs % (2 * CH) == 0:
                        pe.wait_ge(max_stacked[g].sem, max_stacked[g].at(it, s))
                    m = s * 2 * UNITS + hs - 2
                    pe.wait_ge(exp_done.sem, exp_done.at(it, m // (2 * UNITS), m % (2 * UNITS)))
                h = 4 * g + 2 * (hs % 2) + half
                ins = pe.matmul(s2_bank[hs % 2][:, half, :], kst[s % RING][:, h, c * P:(c + 1) * P], qst[s % RING][:, h, :],
                                start=True, stop=True)
                if half == 1:
                    ins.then_inc(s2_done.sem, 1)

            def weigh_values(it, s, u):
                g, c = u // CH, u % CH
                pe.wait_ge(exp_done.sem, exp_done.at(it, s, 2 * u + 1))
                if c == 0:
                    if g:
                        pe.wait_ge(ctx_out.sem, ctx_out.at(it, s, 0))
                    else:
                        pe.wait_ge(ctx_out.sem, ctx_out.at(it, s - 1, 1))
                        pe.wait_ge(v_ready.sem, v_ready.at(it, s))
                for j in range(4):
                    ins = pe.matmul(ctx_bank[32 * j:32 * j + 32, :], vaug[s % RING][:, c, 4 * g + j, :], prob[(UNITS * s + u) % PRING][:, j, :],
                                    start=(c == 0), stop=(c == CH - 1))
                ins.then_inc(pv_done.sem, 1)

            def turn_max(it, s, g):
                shared(it, max_row, s, g)
                pe.wait_ge(max_split.sem, max_split.at(it, s, 2 * g + 1))
                for c in range(CH):
                    ins = pe.transpose(misc.bitcast(BF16)[0:8, c * P:(c + 1) * P], nm[g][:, c].rearrange("p a h -> p (a h)"), identb[:])
                ins.then_inc(max_turned.sem, 1)

            def turn_context(it, s, g):
                shared(it, ctx_norm, s, g)
                pe.wait_ge(ctx_out.sem, ctx_out.at(it, s, g))
                transposes(ctxu[g]).then_inc(ctx_turned.sem, 1)

            def turn_back(it, s):
                shared(it, ctxT_ready, s)
                pe.wait_ge(ctx_norm.sem, ctx_norm.at(it, s, 1))
                transposes(ctxn[:].rearrange("p c n -> p (c n)")).then_inc(ctx_back.sem, 1)

            def project_out(it, s):
                shared(it, node_ready, s)
                pe.wait_ge(ctxT_ready.sem, ctxT_ready.at(it, s))
                pe.matmul(misc, w["wo"][:, node_of(s), :], ctxT[:], start=True, stop=True).then_inc(o_raw.sem, 1)

            def keys(it, s):
                c = node_of(s)
                n = WIRING[c][1][1]
                shared(it, k_ready, s)
                wait_node(pe, it, s, n)
                pe.matmul(misc, w["wk"][:, c, :], tile(s, n)[:], start=True, stop=True).then_inc(k_raw.sem, 1)

            def node_queries(it, s):
                c = node_of(s)
                n = WIRING[c][1][0]
                shared(it, q_ready, s)
                wait_node(pe, it, s, n)
                pe.matmul(misc, w["wqe"][:, c, :], tile(s, n)[:], start=True, stop=True).then_inc(q_raw.sem, 1)

            def head_queries(it, s):
                c = node_of(s)
                shared(it, qq_ready, s)
                pe.wait_ge(q_ready.sem, q_ready.at(it, s))
                pe.matmul(misc, w["wq"][:, c, :], tile(s, c)[:], start=True, stop=True).then_inc(qq_raw.sem, 1)

            def values(it, s):
                c = node_of(s)
                n = WIRING[c][1][2]
                shared(it, v_ready, s)
                wait_node(pe, it, s, n)
                for k in range(CH):
                    ins = pe.matmul(misc[:, k * D:(k + 1) * D], tile(s, n)[:, k * P:(k + 1) * P], w["wv"][:, c, :], start=True, stop=True)
                ins.then_inc(v_raw.sem, 1)

            def output(it, s):
                shared(it, o_copied, lane(s))
                pe.wait_ge(node_ready.sem, node_ready.at(it, s))
                transposes(tile(s, NODES - 1)).then_inc(o_turned.sem, 1)

            def time(it, t, valid):
                if t == 1:
                    free[0] = (v_ready, LANES - 1, 0)
                for hs in range(2 * UNITS):
                    for half in range(2):
                        if valid(t + 1) and hs % 2 == 0:
                            scores_by_query(it, t + 1, hs, half)
                        if valid(t):
                            scores_by_key(it, t, hs, half)
                        if valid(t + 1) and hs % 2 == 1:
                            scores_by_query(it, t + 1, hs, half)
                    if hs % 2 == 1:
                        if hs > 1 and valid(t):
                            weigh_values(it, t, hs // 2 - 1)
                        if hs == 1 and t >= 1:
                            weigh_values(it, t - 1, UNITS - 1)
                    if hs == 1 and valid(t + 3):
                        keys(it, t + 3)
                    if hs == 2 and valid(t):
                        turn_max(it, t, 1)
                    if hs == 4 and t >= 1:
                        turn_context(it, t - 1, 1)
                    if hs == 5 and INPUT + 1 <= t < INPUT + 1 + LANES and valid(SLOTS):
                        first_node(it, LANES + t - INPUT - 1)
                    if hs == 6 and t >= 1:
                        turn_back(it, t - 1)
                    if hs == 8 and t >= 1:
                        project_out(it, t - 1)
                    if hs == 9 and valid(t + 1):
                        turn_max(it, t + 1, 0)
                    if hs == 10 and valid(t + 3):
                        node_queries(it, t + 3)
                    if hs == 11 and t >= 1 and last_node(t - 1):
                        output(it, t - 1)
                    if hs == 12 and valid(t + 3):
                        head_queries(it, t + 3)
                    if hs == 13 and valid(t):
                        turn_context(it, t, 0)
                    if hs == 14 and valid(t + 3):
                        values(it, t + 3)

            run(pe, first_node, time)


def build(nc, a, out):
    mod_rows = nc.dram_tensor("mod_rows", (B, 6 * D), FP32, kind="Internal").ap()
    x_mid = nc.dram_tensor("x_mid", (B, T, D), FP32, kind="Internal").ap()
    modulation_phase(nc, a, mod_rows)
    decay_attention_phase(nc, a, mod_rows, x_mid)
    ctx = ExitStack()
    with ctx:
        w = {n: ctx.enter_context(nc.sbuf_tensor("chain_" + n, [P, NODES, D], FP32)) for n in ("wqe", "wq", "wk", "wv", "wo")}
        w |= {n: ctx.enter_context(nc.sbuf_tensor("chain_" + n, [P, NODES], FP32)) for n in ("bq", "bk", "bo", "eq")}
        chain_weights(nc, a, w)
        node_chain_phase(nc, a, w, mod_rows, x_mid, out)


_ATTN = ["x", "q_w", "q_b", "k_w", "k_b", "v_w", "v_b", "o_w", "o_b", "ln1_w", "ln1_b", "ln2_w", "ln2_b",
         "dec_w", "dec_b", "f1_w", "f1_b", "f2_w", "f2_b"]
_CHAIN = ["ew", "act_w", "We", "be", "Wq", "Wk", "Wv", "Wo", "ln_g", "ln_b"]


def constants():
    p = np.arange(P)
    c = {"c_ident": np.eye(P), "c_upto": p[:, None] <= p[None, :], "c_after": p[:, None] > p[None, :],
         "c_headmask": p[:, None] // LK == np.arange(LH)}
    c["c_blockmask"] = np.repeat(c["c_headmask"][:, :, None], LW, 2)
    c["c_pick"] = np.arange(96)[:, None] % 32 == np.arange(LH)
    c = {k: np.ascontiguousarray(v, dtype=np.float32) for k, v in c.items()}
    return c


def kernel(**inputs):
    import concourse.bacc as bacc
    from concourse.bass_utils import run_bass_kernel_spmd

    nc = bacc.Bacc("TRN2", target_bir_lowering=False, num_devices=1)
    given = {n: inputs["L0_attn_" + n] for n in _ATTN}
    given |= {n: inputs["L0_ffn_" + n] for n in _CHAIN}
    given |= {"c": inputs["L0_c"], "wmod": inputs["L0_wmod"]}
    given |= constants()
    arrays, aps = {}, {}
    for name, value in given.items():
        arrays[f"in_{name}"] = v = np.ascontiguousarray(value)
        aps[name] = nc.dram_tensor(f"in_{name}", v.shape, mybir.dt.from_np(v.dtype), kind="ExternalInput").ap()
    out = nc.dram_tensor("out", (B, T, D), FP32, kind="ExternalOutput").ap()
    build(nc, aps, out)
    r = run_bass_kernel_spmd(nc, [arrays], core_ids=[0])
    return r.results[0]["out"]
```
